# Optimizing a Trainium2 kernel written in Bass

```python
import numpy as np
import jax
import jax.numpy as jnp

def _softmax(x, axis=-1):
    return jax.nn.softmax(x, axis=axis)

def _gelu(x):
    return jax.nn.gelu(x, approximate=True)

def _silu(x):
    return jax.nn.silu(x)

def _sigmoid(x):
    return jax.nn.sigmoid(x)

def _layernorm(x, axis=-1, eps=1e-05):
    m = jnp.mean(x, axis=axis, keepdims=True)
    v = jnp.var(x, axis=axis, keepdims=True)
    return (x - m) / jnp.sqrt(v + eps)

def _scatter_add(tgt, idx, src, axis=0):
    return tgt.at[idx].add(src)

def _segment_sum(src, seg, n):
    return jax.ops.segment_sum(src, seg, n)
kernel_name = 'mk_gnn_preln_d1_gnn_r8_c5ca94'

def setup_inputs(seed: int=0):
    np.random.seed(seed)
    _w = jnp.asarray

    def _rec_inputs():
        import jax
        import jax.numpy as jnp
        _gk = jax.random.key(seed)
        x = -0.0008691 + 1 * jax.random.normal(jax.random.fold_in(_gk, 1), (6250, 128), jnp.float32)
        _s = jax.random.randint(jax.random.fold_in(_gk, 2), (100000,), 0, 6250, jnp.int32)
        _d = jax.random.randint(jax.random.fold_in(_gk, 3), (100000,), 0, 6250, jnp.int32)
        _loop = jnp.arange(6250, dtype=jnp.int32)
        src = jnp.concatenate([_s, _d, _loop])
        dst = jnp.concatenate([_d, _s, _loop])
        _o = jnp.argsort(dst, stable=True)
        src = src[_o]
        dst = dst[_o]
        edge_attr_128 = -8.513e-05 + 0.999844 * jax.random.normal(jax.random.fold_in(_gk, 12), (206250, 128), jnp.float32)
        return (x, src, dst, edge_attr_128)
    x, src, dst, edge_attr_128 = _rec_inputs()

    def _L0_gnn_setup():
        import jax, jax.numpy as jnp
        import numpy as np
        N_NODES = 1250
        N_EDGES = 80000
        D = 128
        BN_EPS = 1e-05

        def _batchnorm(x, gamma, beta):
            mu = jnp.mean(x, axis=0)
            var = jnp.mean(jnp.square(x - mu), axis=0)
            return (x - mu) * jax.lax.rsqrt(var + BN_EPS) * gamma + beta
        key = jax.random.key(seed)
        ks = jax.random.split(key, 8)
        node_feats = jax.random.normal(ks[0], (N_NODES, D), dtype=jnp.float32)
        edge_feats = jax.random.normal(ks[1], (N_EDGES, D), dtype=jnp.float32)
        src = jax.random.randint(ks[2], (N_EDGES,), 0, N_NODES)
        dst = jax.random.randint(ks[3], (N_EDGES,), 0, N_NODES)
        W1 = jax.random.normal(ks[4], (D, 2 * D), dtype=jnp.float32) * (1.0 / np.sqrt(D))
        b1 = jnp.zeros((2 * D,), dtype=jnp.float32)
        gamma1 = jnp.ones((2 * D,), dtype=jnp.float32)
        beta1 = jnp.zeros((2 * D,), dtype=jnp.float32)
        W2 = jax.random.normal(ks[5], (2 * D, D), dtype=jnp.float32) * (1.0 / np.sqrt(2 * D))
        b2 = jnp.zeros((D,), dtype=jnp.float32)
        gamma2 = jnp.ones((D,), dtype=jnp.float32)
        beta2 = jnp.zeros((D,), dtype=jnp.float32)
        eps = jnp.zeros((1,), dtype=jnp.float32)
        return {'node_feats': node_feats, 'edge_feats': edge_feats, 'eps': eps, 'W1': W1, 'b1': b1, 'gamma1': gamma1, 'beta1': beta1, 'W2': W2, 'b2': b2, 'gamma2': gamma2, 'beta2': beta2, 'src': src, 'dst': dst}
    _L0_gnn_all = _L0_gnn_setup()
    _L0_gnn_in = {k: v for k, v in _L0_gnn_all.items() if k in ('eps', 'W1', 'b1', 'gamma1', 'beta1', 'W2', 'b2', 'gamma2', 'beta2')}
    del _L0_gnn_all
    return {'x': x, 'src': src, 'dst': dst, 'edge_attr_128': edge_attr_128, 'L0_gnn_eps': _L0_gnn_in['eps'], 'L0_gnn_W1': _L0_gnn_in['W1'], 'L0_gnn_b1': _L0_gnn_in['b1'], 'L0_gnn_gamma1': _L0_gnn_in['gamma1'], 'L0_gnn_beta1': _L0_gnn_in['beta1'], 'L0_gnn_W2': _L0_gnn_in['W2'], 'L0_gnn_b2': _L0_gnn_in['b2'], 'L0_gnn_gamma2': _L0_gnn_in['gamma2'], 'L0_gnn_beta2': _L0_gnn_in['beta2']}

def reference(x, src, dst, edge_attr_128, L0_gnn_eps, L0_gnn_W1, L0_gnn_b1, L0_gnn_gamma1, L0_gnn_beta1, L0_gnn_W2, L0_gnn_b2, L0_gnn_gamma2, L0_gnn_beta2):
    import jax
    import jax.numpy as jnp

    def _L0_gnn_ref(node_feats, edge_feats, eps, W1, b1, gamma1, beta1, W2, b2, gamma2, beta2, src, dst):
        import jax, jax.numpy as jnp
        import numpy as np
        N_NODES = 1250
        N_EDGES = 80000
        D = 128
        BN_EPS = 1e-05

        def _batchnorm(x, gamma, beta):
            mu = jnp.mean(x, axis=0)
            var = jnp.mean(jnp.square(x - mu), axis=0)
            return (x - mu) * jax.lax.rsqrt(var + BN_EPS) * gamma + beta
        n = node_feats.shape[0]
        m = node_feats[src] + edge_feats
        summed = jax.ops.segment_sum(m, dst, num_segments=n)
        deg = jax.ops.segment_sum(jnp.ones((m.shape[0],), dtype=m.dtype), dst, num_segments=n)
        hv_new = summed / jnp.maximum(deg, 1.0)[:, None]
        h = (1.0 + eps[0]) * node_feats + hv_new
        h = h @ W1 + b1
        h = jax.nn.relu(_batchnorm(h, gamma1, beta1))
        h = h @ W2 + b2
        h = jax.nn.relu(_batchnorm(h, gamma2, beta2))
        return h
    h = jnp.maximum(_layernorm(x, axis=-1), 0.0)
    x = x + _L0_gnn_ref(h, edge_attr_128, L0_gnn_eps, L0_gnn_W1, L0_gnn_b1, L0_gnn_gamma1, L0_gnn_beta1, L0_gnn_W2, L0_gnn_b2, L0_gnn_gamma2, L0_gnn_beta2, src, dst)
    return x

_drawn_inputs = setup_inputs


def setup_inputs(seed=0):
    import zlib

    import numpy as np

    out = dict(_drawn_inputs(seed))
    spreads = {'L0_gnn_b1': (0.0, 0.1),
     'L0_gnn_gamma1': (1.0, 0.2),
     'L0_gnn_beta1': (0.0, 0.1),
     'L0_gnn_b2': (0.0, 0.1),
     'L0_gnn_gamma2': (1.0, 0.2),
     'L0_gnn_beta2': (0.0, 0.1)}
    factors = {}
    for name, (base, spread) in spreads.items():
        noise = np.random.default_rng([zlib.crc32(name.encode()), seed]).standard_normal(out[name].shape)
        drawn = base * np.exp(spread * noise) if base else spread * noise
        out[name] = jnp.asarray(drawn.astype(out[name].dtype))
    for name, factor in factors.items():
        out[name] = (out[name] * factor).astype(out[name].dtype)
    return out
```

```python
import concourse.bass as bass
from concourse import mybir
from contextlib import ExitStack

F32 = mybir.dt.float32
I32 = mybir.dt.int32
ALU = mybir.AluOpType
ACT = mybir.ActivationFunctionType
AX = mybir.AxisListType


def gnn_layer(nc, x, src, dst, edge, eps, W1, b1, gamma1, beta1, W2, b2, gamma2, beta2, out, h_rows):
    P = 128
    N, D = x.shape
    E = src.shape[0]
    F = W1.shape[1]
    FC = F // P
    NBLK = -(-N // P)
    NREST = N - (NBLK - 1) * P
    K = 16
    GE = K * P
    NG = E // GE
    TAIL = E - NG * GE
    TT = -(-TAIL // P)
    TREST = TAIL - (TT - 1) * P
    NT = NG * K + TT
    NCH = -(-NT // P)
    NTP = NCH * P
    NGP = NTP // K
    FULLT = E // P
    CROW = FULLT - (NCH - 1) * P
    W = 80
    NB = 4
    NACC = NBLK * P + P
    PAD = 1.0e6
    Q = 512
    NQ = -(-N // Q)
    LN_EPS = 1e-5

    ctx = ExitStack()
    with ctx:
        def sb(name, shape, dt=F32):
            return ctx.enter_context(nc.sbuf_tensor(name, shape, dt))

        def sem(name):
            return ctx.enter_context(nc.semaphore(name))

        xs = sb("xs", [P, NBLK, D])
        hT = sb("hT", [P, NBLK * P])
        acc = sb("acc", [P, 2, NACC])
        stage = sb("stage", [P, 2 * NB * K * D])
        ebuf = stage[:, 0:NB * K * D].rearrange("p (b k d) -> p b k d", b=NB, k=K)
        gbuf = stage[:, NB * K * D:].rearrange("p (b k d) -> p b k d", b=NB, k=K)
        y1 = stage[:, 0:FC * NQ * Q].rearrange("p (c n) -> p c n", c=FC)
        y2 = acc[:, 1, :]
        hs = stage[:, 0:NBLK * D].rearrange("p (i d) -> p i d", i=NBLK)
        raw_i = stage[:, 8192:8192 + 2 * NCH * P].bitcast(I32).rearrange("p (a c e) -> p a c e", a=2, c=NCH)
        raw_f = stage[:, 12288:12288 + 2 * NCH * P].rearrange("p (a c e) -> p a c e", a=2, c=NCH)
        idxT = sb("idxT", [P, 2, NTP])
        rel = sb("rel", [P, NTP])
        base_f = sb("base_f", [P, NGP])
        base_i = sb("base_i", [P, NGP], I32)
        idx_ring = sb("idx_ring", [P, NB, K], I32)
        onehot = sb("onehot", [P, 2, K, P])
        chk = onehot[:, :, :, :].rearrange("p a k w -> p (a k w)")
        iota = sb("iota", [P, P])
        ident = sb("ident", [P, P])
        ones = sb("ones", [P, P])
        row0 = sb("row0", [P, P])
        stats = sb("stats", [P, NBLK, 6])
        mv = sb("mv", [P, NBLK, 2])
        rstd = sb("rstd", [P, NBLK])
        nmr = sb("nmr", [P, NBLK])
        eps_c = sb("eps_c", [P, 1])
        viol = sb("viol", [P, 2])
        flag = sb("flag", [P, 1], I32)
        w1s = sb("w1s", [P, F])
        w2s = sb("w2s", [P, FC, D])
        prm = sb("prm", [P, 9])
        epsb = sb("epsb", [P, 1])
        bstat = sb("bstat", [P, FC, NQ, 6])
        bmv = sb("bmv", [P, FC, 2])
        bsc = sb("bsc", [P, FC, 3])
        otile = acc[:, 0, 0:NBLK * P].rearrange("p (i d) -> p i d", d=D)
        wbase = sb("wbase", [P, NBLK])
        bank = [ctx.enter_context(nc.psum_tensor(f"bank{i}", [P, Q], F32)) for i in range(8)]
        ps_sum = [bank[0], bank[1]]
        ps_deg = [bank[2], bank[3]]

        x_in, idx_in, prm_in = sem("x_in"), sem("idx_in"), sem("prm_in")
        const_ok = sem("const_ok")
        c_fill = sem("c_fill")
        pads = sem("pads")
        dve = sem("dve_step")
        act = sem("act_step")
        pe = sem("pe_step")
        h_out = sem("h_out")
        setup_done = sem("setup_done")
        slot_free = sem("slot_free")
        e_landed = [sem(f"e_landed{i}") for i in range(NB)]
        g_landed = [sem(f"g_landed{i}") for i in range(NB)]
        idx_ready = sem("idx_ready")
        oh_ready = sem("oh_ready")
        ps_free = sem("ps_free")
        passed = [sem(f"passed{i}") for i in range(3)]
        sl = {n: sem("slow_" + n) for n in ("loaded", "gathered", "idx", "onehot", "mm", "added")}
        mlp_mm, mlp_ev, mlp_dve, mlp_norm, mlp_out, o_ready = (sem(n) for n in (
            "mlp_mm", "mlp_ev", "mlp_dve", "mlp_norm", "mlp_out", "o_ready"))
        tp_ready = sem("tp_ready")
        y_norm = sem("y_norm")
        act_sq = sem("act_sq")
        chain = sem("chain")
        tail_zeroed = sem("tail_zeroed")
        z_ready = sem("z_ready")
        tail_done = sem("tail_done")
        sl["step"] = sem("slow_step")
        sl["added2"] = sem("slow_added_tail")

        block = ctx.enter_context(nc.Block())
        edge_g = edge[0:NG * GE, :].rearrange("(g k p) d -> g p k d", k=K, p=P)

        TPB = Q // P
        HB = [list(range(i, min(i + TPB, NBLK))) for i in range(0, NBLK, TPB)]
        IB = [(a, list(range(i, min(i + TPB, NCH)))) for a in range(2) for i in range(0, NCH, TPB)]

        def edge_load(sp, b, g, landed):
            for h in range(2):
                ks = slice(h * K // 2, (h + 1) * K // 2)
                sp.dma_start(ebuf[:, b, ks, :], edge_g[bass.ds(g, 1), :, ks, :].rearrange("g p k d -> (g p) k d")).then_inc(landed, 16)

        def tail_load(sp, landed):
            sp.dma_start(ebuf[:, 0, 0:TT - 1, :], edge[NG * GE:NG * GE + (TT - 1) * P, :].rearrange("(k p) d -> p k d", p=P)).then_inc(landed, 16)
            sp.dma_start(ebuf[0:TREST, 0, TT - 1, :], edge[NG * GE + (TT - 1) * P:E, :]).then_inc(landed, 16)

        @block.sync
        def _(sp):
            sp.wait_ge(pads, 2)
            for a, v in enumerate((src, dst)):
                full = (NCH - 1) * P * P
                sp.dma_start(raw_i[:, a, 0:NCH - 1, :], v[0:full].rearrange("(c p e) -> p c e", p=P, e=P)).then_inc(idx_in, 16)
                sp.dma_start(raw_i[0:CROW, a, NCH - 1, :], v[full:full + CROW * P].rearrange("(p e) -> p e", e=P)).then_inc(idx_in, 16)
                sp.dma_start(raw_i[CROW:CROW + 1, a, NCH - 1, 0:TREST], v[FULLT * P:E].rearrange("(p e) -> p e", p=1)).then_inc(idx_in, 16)
            sp.dma_start(xs[:, 0:NBLK - 1, :], x[0:(NBLK - 1) * P, :].rearrange("(i p) d -> p i d", p=P)).then_inc(x_in, 16)
            sp.dma_start(xs[0:NREST, NBLK - 1, :], x[(NBLK - 1) * P:N, :]).then_inc(x_in, 16)
            sp.dma_start(w1s[:, :], W1).then_inc(prm_in, 16)
            sp.dma_start(w2s[:, :, :], W2.rearrange("(c p) d -> p c d", p=P)).then_inc(prm_in, 16)
            with nc.allow_non_contiguous_dma(reason="short parameter vectors"):
                for j, v in enumerate((b1, gamma1, beta1)):
                    sp.dma_start(prm[:, FC * j:FC * j + FC], v.rearrange("(c p) -> p c", p=P)).then_inc(prm_in, 16)
                for j, v in enumerate((b2, gamma2, beta2)):
                    sp.dma_start(prm[:, 3 * FC + j:3 * FC + j + 1], v.rearrange("(p c) -> p c", c=1)).then_inc(prm_in, 16)
                sp.dma_start(epsb[:, :], eps.rearrange("(p c) -> p c", c=1).to_broadcast([P, 1])).then_inc(prm_in, 16)
            sp.wait_ge(act, 1)
            sp.dma_start(h_rows[0:(NBLK - 1) * P, :].rearrange("(i p) d -> p i d", p=P), hs[:, 0:NBLK - 1, :]).then_inc(h_out, 16)
            sp.dma_start(h_rows[(NBLK - 1) * P:N, :], hs[0:NREST, NBLK - 1, :]).then_inc(h_out, 16)
            sp.wait_ge(h_out, 32)
            sp.wait_ge(setup_done, 2)
            slow = sp.value_load(flag[0:1, 0:1], min_val=0, max_val=E)
            with sp.If(slow < 1):
                with sp.Fori(0, NG // NB) as it:
                    for b in range(NB):
                        sp.wait_ge(slot_free, it * NB + b + 1)
                        sp.sem_inc(passed[0], 1)
                        edge_load(sp, b, it * NB + b, e_landed[b])
                sp.wait_ge(tail_zeroed, 1)
                tail_load(sp, e_landed[0])
            with sp.Else():
                with sp.Fori(0, NG) as g:
                    sp.wait_ge(sl["added"], g * (NBLK) + 1)
                    sp.sem_inc(passed[0], 1)
                    edge_load(sp, 0, g, sl["loaded"])
                sp.wait_ge(sl["added"], NG * NBLK + 2)
                tail_load(sp, sl["loaded"])
            for i in range(len(HB)):
                sp.wait_ge(o_ready, i + 1)
                lo, n = HB[i][0], len(HB[i])
                if HB[i][-1] == NBLK - 1:
                    n -= 1
                    sp.dma_start(out[(NBLK - 1) * P:N, :], otile[0:NREST, NBLK - 1, :]).then_inc(mlp_out, 16)
                if n:
                    sp.dma_start(out[lo * P:(lo + n) * P, :].rearrange("(i p) d -> p i d", p=P), otile[:, lo:lo + n, :]).then_inc(mlp_out, 16)
            sp.wait_ge(mlp_out, 16 * (len(HB) + (1 if len(HB[-1]) > 1 else 0)))

        def gathers(gp, b, tiles, landed):
            for k in range(tiles):
                gp.indirect_dma_start(gbuf[:, b, k, :], None, h_rows[:, :],
                                      bass.IndirectOffsetOnAxis(ap=idx_ring[:, b, k:k + 1], axis=0)).then_inc(landed, 16)

        @block.gpsimd
        def _(gp):
            nc.gpsimd.iota(iota[:, :], [[1, P]], base=0, channel_multiplier=0, allow_small_or_imprecise_dtypes=True).then_inc(const_ok, 1)
            nc.gpsimd.iota(wbase[:, :], [[P, NBLK]], base=0, channel_multiplier=0, allow_small_or_imprecise_dtypes=True).then_inc(const_ok, 1)
            nc.gpsimd.memset(ones[:, :], 1.0).then_inc(c_fill, 1)
            gp.wait_ge(c_fill, 1)
            nc.gpsimd.affine_select(out=ident[:, :], in_=ones[:, :], compare_op=ALU.is_equal, fill=0.0, base=0,
                                    pattern=[[-1, P]], channel_multiplier=1).then_inc(const_ok, 1)
            nc.gpsimd.affine_select(out=row0[:, :], in_=ones[:, :], compare_op=ALU.is_equal, fill=0.0, base=0,
                                    pattern=[[0, P]], channel_multiplier=1).then_inc(const_ok, 1)
            gp.wait_ge(h_out, 32)
            gp.wait_ge(setup_done, 2)
            slow = gp.value_load(flag[0:1, 0:1], min_val=0, max_val=E)
            with gp.If(slow < 1):
                with gp.Fori(0, NG // NB) as it:
                    for b in range(NB):
                        gp.wait_ge(idx_ready, it * NB + b + 1)
                        gp.sem_inc(passed[1], 1)
                        gathers(gp, b, K, g_landed[b])
                gp.wait_ge(idx_ready, NG + 1)
                gathers(gp, 0, TT, g_landed[0])
            with gp.Else():
                with gp.Fori(0, NG) as g:
                    gp.wait_ge(sl["idx"], g + 1)
                    gp.sem_inc(passed[1], 1)
                    gathers(gp, 0, K, sl["gathered"])
                gp.wait_ge(sl["idx"], NG + 1)
                gathers(gp, 0, TT, sl["gathered"])

        @block.scalar
        def _(ac):
            ac.wait_ge(dve, 1)
            nc.scalar.activation(rstd[:, :], mv[:, :, 1], ACT.Sqrt, bias=eps_c[:, :], scale=1.0).then_inc(act_sq, 1)
            ac.wait_ge(dve, 2)
            for i in range(NBLK):
                last = nc.scalar.activation(hs[:, i, :], xs[:, i, :], ACT.Relu, bias=nmr[:, i:i + 1], scale=rstd[:, i:i + 1])
            last.then_inc(act, 1)
            ac.wait_ge(mlp_dve, 1)
            nc.scalar.activation(bsc[:, :, 2], bmv[:, :, 1], ACT.Sqrt, bias=eps_c[:, :], scale=1.0).then_inc(act_sq, 1)
            ac.wait_ge(mlp_dve, 2)
            for q in range(NQ):
                for c in range(FC):
                    n = min(Q, N - q * Q)
                    nc.scalar.activation(y1[:, c, q * Q:q * Q + n], y1[:, c, q * Q:q * Q + n], ACT.Relu,
                                         bias=bsc[:, c, 1:2], scale=bsc[:, c, 0:1]).then_inc(y_norm, 1)
            ac.wait_ge(mlp_dve, 3)
            nc.scalar.activation(bsc[:, 0:1, 2], bmv[:, 0:1, 1], ACT.Sqrt, bias=eps_c[:, :], scale=1.0).then_inc(act_sq, 1)
            ac.wait_ge(mlp_dve, 4)
            for q in range(NQ):
                n = min(Q, N - q * Q)
                nc.scalar.activation(y2[:, q * Q:q * Q + n], y2[:, q * Q:q * Q + n], ACT.Relu,
                                     bias=bsc[:, 0, 1:2], scale=bsc[:, 0, 0:1]).then_inc(y_norm, 1)

        @block.vector
        def _(ve):
            n_chain = [0]

            def link(ins):
                n_chain[0] += 1
                ins.then_inc(chain, 1)
                ve.wait_ge(chain, n_chain[0])

            nc.vector.memset(xs[:, NBLK - 1, :], 0.0).then_inc(pads, 1)
            nc.vector.memset(raw_i[:, 0, NCH - 1, :], 0)
            nc.vector.memset(raw_i[:, 1, NCH - 1, :], int(PAD)).then_inc(pads, 1)
            nc.vector.memset(eps_c[:, :], LN_EPS)
            nc.vector.memset(acc[:, :, :], 0.0)
            ve.wait_ge(x_in, 32)
            for i in range(NBLK):
                last = nc.vector.bn_stats(stats[:, i, :], xs[:, i, :])
            link(last)
            for i in range(NBLK):
                last = nc.vector.bn_aggr(mv[:, i, :], stats[:, i, :])
            last.then_inc(dve, 1)
            ve.wait_ge(act_sq, 1)
            link(nc.vector.reciprocal(rstd[:, :], rstd[:, :]))
            nc.vector.scalar_tensor_tensor(out=nmr[:, :], in0=mv[:, :, 0], scalar=-1.0, in1=rstd[:, :],
                                           op0=ALU.mult, op1=ALU.mult).then_inc(dve, 1)
            ve.wait_ge(idx_in, 96)
            nc.vector.tensor_copy(raw_f[:, :, :, :], raw_i[:, :, :, :]).then_inc(dve, 1)
            n = 0
            for a, cs in IB:
                n += 1
                ve.wait_ge(pe, n)
                w = len(cs) * P
                last = nc.vector.tensor_copy(idxT[:, a, cs[0] * P:cs[0] * P + w], bank[4 + n % 4][:, 0:w])
                last.then_inc(dve, 1)
            ve.wait_ge(pe, n + 1)
            nc.vector.tensor_copy(base_i[:, :], bank[0][:, 0:NGP])
            link(nc.vector.tensor_copy(base_f[:, :], bank[0][:, 0:NGP]))
            link(nc.vector.tensor_tensor(rel[:, :].rearrange("p (g k) -> p g k", k=K), idxT[:, 1, :].rearrange("p (g k) -> p g k", k=K),
                                         base_f[:, :].unsqueeze(2).to_broadcast([P, NGP, K]), ALU.subtract))
            link(nc.vector.tensor_scalar(chk[:, 0:NT], rel[:, 0:NT], float(W), None, ALU.is_ge))
            link(nc.vector.scalar_tensor_tensor(out=chk[:, 0:NT], in0=rel[:, 0:NT], scalar=PAD / 2, in1=chk[:, 0:NT],
                                                op0=ALU.is_lt, op1=ALU.mult))
            link(nc.vector.scalar_tensor_tensor(out=chk[:, 0:NT], in0=rel[:, 0:NT], scalar=0.0, in1=chk[:, 0:NT],
                                                op0=ALU.is_lt, op1=ALU.add))
            nc.vector.tensor_reduce(viol[:, 0:1], chk[:, 0:NT], axis=AX.X, op=ALU.add).then_inc(dve, 1)
            ve.wait_ge(pe, n + 2)
            nc.vector.tensor_copy(flag[:, :], bank[1][:, 0:1])
            m = n + 2
            for i, blks in enumerate(HB):
                m += 1
                ve.wait_ge(pe, m)
                w = len(blks) * P
                last = nc.vector.tensor_copy(hT[:, blks[0] * P:blks[0] * P + w], bank[4 + m % 4][:, 0:w])
                last.then_inc(dve, 1)
            nc.vector.memset(viol[:, 1:2], 0.0).then_inc(setup_done, 2)

            def build(slot, oh, col, tiles, width, r):
                return nc.vector.tensor_tensor(
                    onehot[:, oh, 0:tiles, 0:width], iota[:, 0:width].unsqueeze(1).to_broadcast([P, tiles, width]),
                    r.unsqueeze(2).to_broadcast([P, tiles, width]), ALU.is_equal)

            def evac(g_base, oh, width):
                nc.vector.tensor_tensor(acc[:, 0, bass.ds(g_base, width)], acc[:, 0, bass.ds(g_base, width)],
                                        ps_sum[oh][:, 0:width], ALU.add)
                return nc.vector.tensor_tensor(acc[:, 1, bass.ds(g_base, width)], acc[:, 1, bass.ds(g_base, width)],
                                               ps_deg[oh][:, 0:width], ALU.add)

            ve.wait_ge(setup_done, 2)
            ve.wait_ge(const_ok, 4)
            slow = ve.value_load(flag[0:1, 0:1], min_val=0, max_val=E)
            with ve.If(slow < 1):
                ve.sem_inc(slot_free, NB)
                ve.sem_inc(ps_free, 2)
                for g in range(2):
                    nc.vector.tensor_copy(idx_ring[:, g, :], idxT[:, 0, g * K:(g + 1) * K]).then_inc(idx_ready, 1)
                build(0, 0, None, K, W, rel[:, 0:K]).then_inc(oh_ready, 1)
                with ve.Fori(0, NG // NB) as it:
                    for b in range(NB):
                        g = it * NB + b
                        ve.wait_ge(slot_free, g + 3)
                        nc.vector.tensor_copy(idx_ring[:, (b + 2) % NB, :],
                                              idxT[:, 0, bass.ds((g + 2) * K, K)]).then_inc(idx_ready, 1)
                        build(b, (b + 1) % 2, None, K, W, rel[:, bass.ds((g + 1) * K, K)]).then_inc(oh_ready, 1)
                        ve.wait_ge(slot_free, g + (NB + 1))
                        base = ve.value_load(base_i[0:1, bass.ds(g, 1)], min_val=0, max_val=N - 1)
                        ve.wait_ge(ps_free, g + 2)
                        evac(base, b % 2, W).then_inc(ps_free, 1)
                nc.vector.memset(ebuf[:, 0, TT - 1, :], 0.0).then_inc(tail_zeroed, 1)
                ve.wait_ge(slot_free, NG + NB + 1)
                base = ve.value_load(base_i[0:1, NG:NG + 1], min_val=0, max_val=N - 1)
                ve.wait_ge(ps_free, NG + 2)
                evac(base, 0, W).then_inc(tail_done, 1)
            with ve.Else():
                ve.sem_inc(sl["added"], 1)

                def windows(g, tiles, dests):
                    with ve.Fori(0, NBLK) as w:
                        nc.vector.tensor_copy(rel[:, 0:tiles], dests).then_inc(sl["step"], 1)
                        ve.wait_ge(sl["step"], (g * NBLK + w) * 2 + 1)
                        nc.vector.tensor_tensor(rel[:, 0:tiles], rel[:, 0:tiles],
                                                wbase[:, bass.ds(w, 1)].to_broadcast([P, tiles]), ALU.subtract).then_inc(sl["step"], 1)
                        ve.wait_ge(sl["step"], (g * NBLK + w) * 2 + 2)
                        build(0, 0, None, tiles, P, rel[:, 0:tiles]).then_inc(sl["onehot"], 1)
                        ve.wait_ge(sl["mm"], g * NBLK + w + 1)
                        evac(w * P, 0, P).then_inc(sl["added"], 1)
                        ve.wait_ge(sl["added"], g * NBLK + w + 2)
                with ve.Fori(0, NG) as g:
                    nc.vector.tensor_copy(idx_ring[:, 0, :], idxT[:, 0, bass.ds(g * K, K)]).then_inc(sl["idx"], 1)
                    windows(g, K, idxT[:, 1, bass.ds(g * K, K)])
                nc.vector.memset(ebuf[:, 0, TT - 1, :], 0.0).then_inc(sl["added"], 1)
                ve.wait_ge(sl["added"], NG * NBLK + 2)
                nc.vector.tensor_copy(idx_ring[:, 0, 0:TT], idxT[:, 0, NG * K:NT]).then_inc(sl["idx"], 1)
                with ve.Fori(0, NBLK) as w:
                    nc.vector.tensor_tensor(rel[:, 0:TT], idxT[:, 1, NG * K:NT],
                                            wbase[:, bass.ds(w, 1)].to_broadcast([P, TT]), ALU.subtract).then_inc(sl["step"], 1)
                    ve.wait_ge(sl["step"], w + (NG * NBLK * 2 + 1))
                    build(0, 0, None, TT, P, rel[:, 0:TT]).then_inc(sl["onehot"], 1)
                    ve.wait_ge(sl["mm"], w + (NG * NBLK + 1))
                    evac(w * P, 0, P).then_inc(sl["added2"], 1)
                    ve.wait_ge(sl["added2"], w + 1)
                ve.sem_inc(tail_done, 1)

            ve.wait_ge(tail_done, 1)
            ve.wait_ge(prm_in, 144)
            link(nc.vector.tensor_scalar(acc[:, 1, 0:N], acc[:, 1, 0:N], 1.0, None, ALU.max))
            link(nc.vector.reciprocal(acc[:, 1, 0:N], acc[:, 1, 0:N]))
            link(nc.vector.tensor_tensor(acc[:, 0, 0:N], acc[:, 0, 0:N], acc[:, 1, 0:N], ALU.mult))
            link(nc.vector.tensor_scalar(epsb[:, :], epsb[:, :], 1.0, None, ALU.add))
            nc.vector.scalar_tensor_tensor(out=acc[:, 0, 0:N], in0=hT[:, 0:N], scalar=epsb[:, :], in1=acc[:, 0, 0:N],
                                           op0=ALU.mult, op1=ALU.add).then_inc(z_ready, 1)

            def scale_shift(c, nch, pg, pb, after, sq):
                link(last_stat[0])
                for cc in range(nch):
                    last_stat[0] = nc.vector.bn_aggr(bmv[:, cc, :], bstat[:, cc, :, :].rearrange("p q s -> p (q s)"))
                last_stat[0].then_inc(mlp_dve, 1)
                ve.wait_ge(act_sq, sq)
                link(nc.vector.reciprocal(bsc[:, 0:nch, 2], bsc[:, 0:nch, 2]))
                link(nc.vector.tensor_tensor(bsc[:, 0:nch, 0], prm[:, pg:pg + nch], bsc[:, 0:nch, 2], ALU.mult))
                link(nc.vector.tensor_tensor(bsc[:, 0:nch, 1], bmv[:, 0:nch, 0], bsc[:, 0:nch, 0], ALU.mult))
                nc.vector.tensor_tensor(bsc[:, 0:nch, 1], prm[:, pb:pb + nch], bsc[:, 0:nch, 1], ALU.subtract).then_inc(mlp_dve, 1)

            last_stat = [None]
            t = 0
            for q in range(NQ):
                for c in range(FC):
                    n = min(Q, N - q * Q)
                    ve.wait_ge(mlp_mm, t + 1)
                    link(nc.vector.tensor_scalar(y1[:, c, q * Q:q * Q + n], bank[t % 8][:, 0:n], prm[:, c:c + 1], None, ALU.add))
                    last_stat[0] = nc.vector.bn_stats(bstat[:, c, q, :], y1[:, c, q * Q:q * Q + n])
                    if t < NQ * FC - 1:
                        last_stat[0].then_inc(mlp_ev, 1)
                    t += 1
            scale_shift(0, FC, FC, 2 * FC, None, 2)
            for q in range(NQ):
                n = min(Q, N - q * Q)
                ve.wait_ge(mlp_mm, t + 1)
                link(nc.vector.tensor_scalar(y2[:, q * Q:q * Q + n], bank[t % 8][:, 0:n], prm[:, 3 * FC:3 * FC + 1], None, ALU.add))
                last_stat[0] = nc.vector.bn_stats(bstat[:, 0, q, :], y2[:, q * Q:q * Q + n])
                if q < NQ - 1:
                    last_stat[0].then_inc(mlp_ev, 1)
                t += 1
            scale_shift(0, 1, 3 * FC + 1, 3 * FC + 2, None, 3)
            for i, blks in enumerate(HB):
                ve.wait_ge(tp_ready, i + 1)
                w = len(blks) * P
                lo = blks[0]
                nc.vector.tensor_tensor(otile[:, lo:lo + len(blks), :], xs[:, lo:lo + len(blks), :],
                                        bank[i % 8][:, 0:w].rearrange("p (i d) -> p i d", d=D), ALU.add).then_inc(o_ready, 1)

        @block.tensor
        def _(te):
            te.wait_ge(const_ok, 4)
            te.wait_ge(dve, 3)
            n = 0
            for a, cs in IB:
                n += 1
                if n > 4:
                    te.wait_ge(dve, 3 + n - 4)
                for j, c in enumerate(cs):
                    last = nc.tensor.transpose(bank[4 + n % 4][:, j * P:(j + 1) * P], raw_f[:, a, c, :], ident[:, :])
                last.then_inc(pe, 1)
            te.wait_ge(dve, 3 + n)
            nc.tensor.matmul(bank[0][:, 0:NGP], row0[:, :], idxT[:, 1, :].rearrange("p (g k) -> p g k", k=K)[:, :, 0],
                             start=True, stop=True).then_inc(pe, 1)
            te.wait_ge(dve, 3 + n + 1)
            nc.tensor.matmul(bank[1][:, 0:1], ones[:, :], viol[:, 0:1], start=True, stop=True).then_inc(pe, 1)
            m = n + 2
            te.wait_ge(act, 1)
            for i, blks in enumerate(HB):
                m += 1
                if i >= 4:
                    te.wait_ge(dve, 3 + n + 1 + i - 3)
                for j, c in enumerate(blks):
                    last = nc.tensor.transpose(bank[4 + m % 4][:, j * P:(j + 1) * P], hs[:, c, :], ident[:, :])
                last.then_inc(pe, 1)

            def group(b, oh, tiles, width):
                for k in range(tiles):
                    o = onehot[:, oh, k, 0:width]
                    nc.tensor.matmul(ps_sum[oh][:, 0:width], ebuf[:, b, k, :], o, start=(k == 0), stop=False)
                    nc.tensor.matmul(ps_sum[oh][:, 0:width], gbuf[:, b, k, :], o, start=False, stop=(k == tiles - 1))
                    last = nc.tensor.matmul(ps_deg[oh][:, 0:width], ones[:, :], o, start=(k == 0), stop=(k == tiles - 1))
                return last

            te.wait_ge(setup_done, 2)
            slow = te.value_load(flag[0:1, 0:1], min_val=0, max_val=E)
            with te.If(slow < 1):
                with te.Fori(0, NG // NB) as it:
                    for b in range(NB):
                        te.wait_ge(e_landed[b], it * 32 + 32)
                        te.wait_ge(g_landed[b], it * (16 * K) + 16 * K)
                        te.wait_ge(oh_ready, it * NB + b + 1)
                        te.wait_ge(ps_free, it * NB + b + 1)
                        group(b, b % 2, K, W).then_inc(slot_free, 1)
                te.wait_ge(e_landed[0], (NG // NB) * 32 + 32)
                te.wait_ge(g_landed[0], (NG // NB) * 16 * K + 16 * TT)
                te.wait_ge(oh_ready, NG + 1)
                te.wait_ge(ps_free, NG + 1)
                group(0, 0, TT, W).then_inc(slot_free, 1)
            with te.Else():
                with te.Fori(0, NG) as g:
                    te.wait_ge(sl["loaded"], g * 32 + 32)
                    te.wait_ge(sl["gathered"], g * (16 * K) + 16 * K)
                    te.sem_inc(passed[2], 1)
                    with te.Fori(0, NBLK) as w:
                        te.wait_ge(sl["onehot"], g * NBLK + w + 1)
                        group(0, 0, K, P).then_inc(sl["mm"], 1)
                te.wait_ge(sl["loaded"], NG * 32 + 32)
                te.wait_ge(sl["gathered"], NG * 16 * K + 16 * TT)
                with te.Fori(0, NBLK) as w:
                    te.wait_ge(sl["onehot"], w + (NG * NBLK + 1))
                    group(0, 0, TT, P).then_inc(sl["mm"], 1)
            te.wait_ge(z_ready, 1)
            t = 0
            for q in range(NQ):
                for c in range(FC):
                    n = min(Q, N - q * Q)
                    if t >= 8:
                        te.wait_ge(mlp_ev, t - 7)
                    nc.tensor.matmul(bank[t % 8][:, 0:n], w1s[:, c * P:(c + 1) * P], acc[:, 0, q * Q:q * Q + n],
                                     start=True, stop=True).then_inc(mlp_mm, 1)
                    t += 1
            for q in range(NQ):
                n = min(Q, N - q * Q)
                te.wait_ge(y_norm, (q + 1) * FC)
                if q >= 8:
                    te.wait_ge(mlp_ev, NQ * FC - 1 + q - 7)
                for c in range(FC):
                    last = nc.tensor.matmul(bank[t % 8][:, 0:n], w2s[:, c, :], y1[:, c, q * Q:q * Q + n],
                                            start=(c == 0), stop=(c == FC - 1))
                last.then_inc(mlp_mm, 1)
                t += 1
            for i, blks in enumerate(HB):
                te.wait_ge(y_norm, NQ * FC + i + 1)
                if i >= 8:
                    te.wait_ge(o_ready, i - 7)
                for j, c in enumerate(blks):
                    w = min(P, N - c * P)
                    last = nc.tensor.transpose(bank[i % 8][0:w, j * P:(j + 1) * P], y2[:, c * P:c * P + w], ident[:, :])
                last.then_inc(tp_ready, 1)


_INS = ['x', 'src', 'dst', 'edge_attr_128', 'L0_gnn_eps', 'L0_gnn_W1', 'L0_gnn_b1', 'L0_gnn_gamma1', 'L0_gnn_beta1',
        'L0_gnn_W2', 'L0_gnn_b2', 'L0_gnn_gamma2', 'L0_gnn_beta2']


def kernel(**inputs):
    import numpy as _np
    import concourse.bacc as _bacc
    from concourse import mybir as _mybir
    from concourse.bass_utils import run_bass_kernel_spmd as _run

    nc = _bacc.Bacc("TRN2", target_bir_lowering=False, num_devices=1)
    arrays, args = {}, []
    for name in _INS:
        a = _np.ascontiguousarray(inputs[name])
        arrays[f"in_{name}"] = a
        args.append(nc.dram_tensor(f"in_{name}", a.shape, _mybir.dt.from_np(a.dtype), kind="ExternalInput").ap())
    shape = inputs['x'].shape
    args.append(nc.dram_tensor("out_x", shape, _mybir.dt.float32, kind="ExternalOutput").ap())
    args.append(nc.dram_tensor("h_rows", shape, _mybir.dt.float32, kind="Internal").ap())
    gnn_layer(nc, *args)
    r = _run(nc, [arrays], core_ids=[0])
    return r.results[0]["out_x"]
```

```python
import concourse.bass as bass
from concourse import mybir
from contextlib import ExitStack

F32 = mybir.dt.float32
I32 = mybir.dt.int32
I16 = mybir.dt.int16
F16 = mybir.dt.float16
BF16 = mybir.dt.bfloat16
ALU = mybir.AluOpType
ACT = mybir.ActivationFunctionType
AX = mybir.AxisListType
PE_ENGINE = mybir.EngineType.PE
DVE_ENGINE = mybir.EngineType.DVE


def gnn_layer(nc, x, src, dst, edge, eps, W1, b1, gamma1, beta1, W2, b2, gamma2, beta2, out, h_rows, tables):
    P = 128
    N, D = x.shape
    E = src.shape[0]
    F = W1.shape[1]
    FC = F // P
    NBLK = -(-N // P)
    NREST = N - (NBLK - 1) * P
    NT = -(-E // P)
    TREST = E - (NT - 1) * P
    NCH = -(-NT // P)
    NTP = NCH * P
    CROW = NT - 1 - (NCH - 1) * P
    PAD = 30000

    SETS, ST, GT = 6, 6, 16
    CT = SETS * ST
    T = CT + GT
    NSTEP = (NT - 1) // T
    TAILG = NT - NSTEP * T - CT
    assert NSTEP % 2 == 0 and 0 < TAILG <= GT
    WT = 7
    WS = 30
    WG = 76
    COVER = 21
    AB = 3
    AR = -(-NBLK // AB)
    RING = 3
    WC = SETS * WS
    NBASE = SETS + 1

    K = 16
    NG = NT // K
    TT = NT - NG * K

    NACC = max(N + 100, NBLK * P)
    Q = 512
    NQ = -(-N // Q)
    LN_EPS = 1e-5

    ctx = ExitStack()
    with ctx:
        def sb(name, shape, dt=F32):
            return ctx.enter_context(nc.sbuf_tensor(name, shape, dt))

        def sem(name):
            return ctx.enter_context(nc.semaphore(name))

        sizes = [RING * ST * D, 2 * GT * D, 2 * GT * D, 2 * NBLK * WC // 2, 2 * ST * AB * AR * WT // 2]
        at = [sum(sizes[:i]) for i in range(len(sizes) + 1)]
        stage = sb("stage", [P, at[-1]])
        e_cnt = stage[:, at[0]:at[1]].rearrange("p (r k d) -> p r k d", r=RING, k=ST)
        e_gat = stage[:, at[1]:at[2]].rearrange("p (b k d) -> p b k d", b=2, k=GT)
        g_gat = stage[:, at[2]:at[3]].rearrange("p (b k d) -> p b k d", b=2, k=GT)
        cnt = stage[:, at[3]:at[4]].bitcast(F16).rearrange("p (b a w) -> p b a w", b=2, a=NBLK)
        zhot = stage[:, at[4]:at[5]].bitcast(F16).rearrange("p (b k w) -> p b k w", b=2, k=ST)
        BD = NBLK * D
        xs = stage[:, 0:BD].rearrange("p (i d) -> p i d", d=D)
        hs = stage[:, BD:2 * BD].rearrange("p (i d) -> p i d", d=D)
        left = stage[:, 2 * BD:3 * BD].rearrange("p (i d) -> p i d", d=D)
        stats = stage[:, 3 * BD:3 * BD + 6 * NBLK].rearrange("p (i s) -> p i s", s=6)
        row0 = stage[:, 3 * BD + 6 * NBLK:3 * BD + 6 * NBLK + P]
        LN = 3 * BD + 6 * NBLK + P
        mv = stage[:, LN:LN + 2 * NBLK].rearrange("p (i s) -> p i s", s=2)
        rstd = stage[:, LN + 2 * NBLK:LN + 3 * NBLK]
        nmr = stage[:, LN + 3 * NBLK:LN + 4 * NBLK]
        y1 = stage[:, 0:FC * NQ * Q].rearrange("p (c n) -> p c n", c=FC)
        hback = stage[:, FC * NQ * Q:FC * NQ * Q + BD].rearrange("p (i d) -> p i d", d=D)
        AFTER = FC * NQ * Q + BD
        w1s = stage[:, AFTER:AFTER + F]
        w2s = stage[:, AFTER + F:AFTER + F + FC * D].rearrange("p (c d) -> p c d", c=FC)
        bstat = stage[:, AFTER + 2 * F:AFTER + 2 * F + FC * NQ * 6].rearrange("p (c q s) -> p c q s", c=FC, q=NQ)
        ebuf = stage[:, at[1]:at[1] + K * D].rearrange("p (k d) -> p k d", k=K)
        gbuf = stage[:, at[2]:at[2] + K * D].rearrange("p (k d) -> p k d", k=K)
        onehot = stage[:, at[3]:at[3] + K * P].rearrange("p (k w) -> p k w", k=K)
        rel_w = stage[:, at[4]:at[4] + K]

        acc = sb("acc", [P, 2, NACC])
        accf = acc[:, :, :].rearrange("p a n -> p (a n)")
        raw_i = accf[:, 0:4 * NTP].bitcast(I32).rearrange("p (a c e) -> p a c e", a=4, c=NCH)
        raw_f = accf[:, NTP:4 * NTP].rearrange("p (a c e) -> p a c e", a=3, c=NCH)
        idxT = accf[:, 4 * NTP:7 * NTP].rearrange("p (a t) -> p a t", a=3)
        tmp = [accf[:, j * NTP:(j + 1) * NTP] for j in range(3)]
        y2 = acc[:, 1, :]
        otile = acc[:, 0, 0:NBLK * P].rearrange("p (i d) -> p i d", d=D)
        hp = sb("hp", [P, 3, NBLK, D], BF16)
        xback = hp[:, :, :, :].rearrange("p a i d -> p (a i d)").bitcast(F32)[:, 0:BD].rearrange("p (i d) -> p i d", d=D)

        sd = hp[:, :, :, :].rearrange("p a i d -> p (a i d)").bitcast(F32)[:, 0:2 * NTP].rearrange("p (a t) -> p a t", a=2)

        key = sb("key", [P, NTP], F16)
        row = sb("row", [P, NTP], BF16)
        rel = sb("rel", [P, NTP], BF16)
        gat_src = sb("gat_src", [P, NSTEP + 1, GT], I16)
        gat_flat = gat_src[:, :, :].rearrange("p i g -> p (i g)")
        off_i = sb("off_i", [P, NTP], I32)
        base_i = sb("base_i", [P, (NSTEP + 1) * NBASE], I32)
        idx_ring = sb("idx_ring", [P, 2, GT], I32)
        rhot = sb("rhot", [P, 2, ST, P], BF16)
        dhot = sb("dhot", [P, 2, T, WT])
        dhot_b = sb("dhot_b", [P, 2, T, WT], BF16)
        e_last = sb("e_last", [P, D])

        zk = sb("zk", [P, AB * AR * WT], F16)
        iota_b = sb("iota_b", [P, P], BF16)
        ident = sb("ident", [P, P])
        ones = sb("ones", [P, P])
        ones_b = sb("ones_b", [P, P], BF16)
        zero_b = sb("zero_b", [P, P], BF16)
        wbase = sb("wbase", [P, NBLK])
        eps_c = sb("eps_c", [P, 1])
        viol = sb("viol", [P, 8])
        flag = sb("flag", [P, 1], I32)
        prm = sb("prm", [P, 9])
        epsb = sb("epsb", [P, 1])
        bmv = sb("bmv", [P, FC, 2])
        bsc = sb("bsc", [P, FC, 3])
        ps = ctx.enter_context(nc.psum_tensor("ps", [P, 8, Q], F32))
        bank = [ps[:, i, :] for i in range(8)]
        set_ps = [[bank[AB * b + j][:, 0:AR * WS].rearrange("p (a w) -> p a w", a=AR) for j in range(AB)] for b in range(2)]
        ed = bank[6].rearrange("p (a n) -> p a n", a=2)
        prod = bank[7][:, 0:WC]
        psf = ps[:, :, :].rearrange("p b n -> p (b n)")

        x_in, idx_in, prm_in = sem("x_in"), sem("idx_in"), sem("prm_in")
        c_fill, const_ok, pads = sem("c_fill"), sem("const_ok"), sem("pads")
        ln_stats, ln_scale, h_done = sem("ln_stats"), sem("ln_scale"), sem("h_done")
        act_sq, h_out, split_done = sem("act_sq"), sem("h_out"), sem("split_done")
        idx_float, idx_bank, idx_taken = sem("idx_float"), sem("idx_bank"), sem("idx_taken")
        firsts, viol_ok, viol_sum = sem("firsts"), sem("viol_ok"), sem("viol_sum")
        tables_ok, tables_out, tables_in = sem("tables_ok"), sem("tables_out"), sem("tables_in")
        setup_done, last_edges = sem("setup_done"), sem("last_edges")
        chain = sem("chain")
        passed = {n: sem("passed_" + n) for n in ("sync", "gpsimd", "tensor", "vector")}

        set_free = sem("set_free")
        hot_ready = sem("hot_ready")
        cnt_ready = sem("cnt_ready")
        ring_free = sem("ring_free")
        cnt_landed = [sem(f"cnt_landed{r}") for r in range(RING)]
        step_summed = sem("step_summed")
        dhot_ready = sem("dhot_ready")
        idx_ready = sem("idx_ready")
        gat_e = [sem(f"gat_e{b}") for b in range(2)]
        gat_h = [sem(f"gat_h{b}") for b in range(2)]
        gat_ready = sem("gat_ready")
        prod_done = sem("prod_done")
        prod_taken = sem("prod_taken")
        ed_taken = sem("ed_taken")
        acc_add = sem("acc_add")
        sums_done = sem("sums_done")

        sl = {n: sem("slow_" + n) for n in ("loaded", "gathered", "idx", "onehot", "mm", "added", "tail", "step")}

        back_in, zT, z_ready = sem("back_in"), sem("zT"), sem("z_ready")
        mm1, y_out, y_stat = sem("mm1"), sem("y_out"), sem("y_stat")
        bn_stat, bn_coef, y_norm = sem("bn_stat"), sem("bn_coef"), sem("y_norm")
        mm2, y2_out, o_T, o_ready, stored = sem("mm2"), sem("y2_out"), sem("o_T"), sem("o_ready"), sem("stored")

        block = ctx.enter_context(nc.Block())

        TPB = Q // P
        HB = [list(range(i, min(i + TPB, NBLK))) for i in range(0, NBLK, TPB)]
        IB = [(a, list(range(i, min(i + TPB, NCH)))) for a in range(3) for i in range(0, NCH, TPB)]

        def steps(eng, body):
            for i in range(2):
                body(i, 0, i, "first" if i == 0 else "whole")
            with eng.Fori(1, NSTEP // 2) as u:
                for b in range(2):
                    body(u * 2 + b, u, b, "whole")
            body(NSTEP, NSTEP // 2, 0, "last")

        @block.sync
        def _(sp):
            sp.wait_ge(pads, 2)
            for a, v in enumerate((src, dst)):
                full = (NCH - 1) * P * P
                sp.dma_start(raw_i[:, a, 0:NCH - 1, :], v[0:full].rearrange("(c p e) -> p c e", p=P, e=P)).then_inc(idx_in, 16)
                sp.dma_start(raw_i[0:CROW, a, NCH - 1, :], v[full:full + CROW * P].rearrange("(p e) -> p e", e=P)).then_inc(idx_in, 16)
                sp.dma_start(raw_i[CROW:CROW + 1, a, NCH - 1, 0:TREST], v[E - TREST:E].rearrange("(p e) -> p e", p=1)).then_inc(idx_in, 16)
            sp.dma_start(xs[:, 0:NBLK - 1, :], x[0:(NBLK - 1) * P, :].rearrange("(i p) d -> p i d", p=P)).then_inc(x_in, 16)
            sp.dma_start(xs[0:NREST, NBLK - 1, :], x[(NBLK - 1) * P:N, :]).then_inc(x_in, 16)
            sp.dma_start(e_last[0:TREST, :], edge[E - TREST:E, :]).then_inc(last_edges, 16)
            with nc.allow_non_contiguous_dma(reason="short parameter vectors"):
                for j, v in enumerate((b1, gamma1, beta1)):
                    sp.dma_start(prm[:, FC * j:FC * j + FC], v.rearrange("(c p) -> p c", p=P)).then_inc(prm_in, 16)
                for j, v in enumerate((b2, gamma2, beta2)):
                    sp.dma_start(prm[:, 3 * FC + j:3 * FC + j + 1], v.rearrange("(p c) -> p c", c=1)).then_inc(prm_in, 16)
                sp.dma_start(epsb[:, :], eps.rearrange("(p c) -> p c", c=1).to_broadcast([P, 1])).then_inc(prm_in, 16)
            sp.wait_ge(h_done, 1)
            sp.dma_start(h_rows[0:(NBLK - 1) * P, :].rearrange("(i p) d -> p i d", p=P), hs[:, 0:NBLK - 1, :]).then_inc(h_out, 16)
            sp.dma_start(h_rows[(NBLK - 1) * P:N, :], hs[0:NREST, NBLK - 1, :]).then_inc(h_out, 16)
            sp.wait_ge(tables_ok, 1)
            sp.dma_start(tables, accf[:, 4 * NTP:6 * NTP]).then_inc(tables_out, 16)
            sp.wait_ge(h_out, 32)
            sp.wait_ge(setup_done, 1)
            slow = sp.value_load(flag[0:1, 0:1], min_val=0, max_val=8 * E)
            with sp.If(slow < 1):
                def load_step(i, u, b, kind):
                    sp.wait_ge(step_summed, i + 1)
                    sp.sem_inc(passed["sync"], 1)
                    lo = i * (T * P) + CT * P
                    if kind == "last":
                        sp.dma_start(e_gat[:, b, 0:TAILG - 1, :], edge[lo:lo + (TAILG - 1) * P, :].rearrange("(k p) d -> p k d", p=P)).then_inc(gat_e[b], 16)
                    else:
                        for h in range(2):
                            n = GT // 2
                            sp.dma_start(e_gat[:, b, h * n:(h + 1) * n, :],
                                         edge[bass.ds(lo + h * n * P, n * P), :].rearrange("(k p) d -> p k d", p=P)).then_inc(gat_e[b], 16)
                    for s in range(SETS):
                        r = (SETS * b + s) % RING
                        sp.wait_ge(ring_free, i * SETS + s + 1)
                        sp.sem_inc(passed["sync"], 1)
                        sp.dma_start(e_cnt[:, r], edge[bass.ds(i * (T * P) + s * ST * P, ST * P), :].rearrange("(k p) d -> p k d", p=P)).then_inc(cnt_landed[r], 16)
                steps(sp, load_step)
            with sp.Else():
                sp.dma_start(sd.rearrange("p a t -> p (a t)"), tables).then_inc(tables_in, 16)
                with sp.Fori(0, NG) as g:
                    sp.wait_ge(sl["added"], g * NBLK + 1)
                    sp.sem_inc(passed["sync"], 1)
                    for h in range(2):
                        n = K // 2
                        sp.dma_start(ebuf[:, h * n:(h + 1) * n, :],
                                     edge[bass.ds(g * (K * P) + h * n * P, n * P), :].rearrange("(k p) d -> p k d", p=P)).then_inc(sl["loaded"], 16)
                sp.wait_ge(sl["added"], NG * NBLK + 2)
                lo = NG * K * P
                sp.dma_start(ebuf[:, 0:TT - 1, :], edge[lo:lo + (TT - 1) * P, :].rearrange("(k p) d -> p k d", p=P)).then_inc(sl["loaded"], 16)
                sp.dma_start(ebuf[0:TREST, TT - 1, :], edge[E - TREST:E, :]).then_inc(sl["loaded"], 16)
            sp.wait_ge(sums_done, 1)
            for v, buf in ((h_rows, hback), (x, xback)):
                sp.dma_start(buf[:, 0:NBLK - 1, :], v[0:(NBLK - 1) * P, :].rearrange("(i p) d -> p i d", p=P)).then_inc(back_in, 16)
                sp.dma_start(buf[0:NREST, NBLK - 1, :], v[(NBLK - 1) * P:N, :]).then_inc(back_in, 16)
            sp.dma_start(w1s, W1).then_inc(back_in, 16)
            sp.dma_start(w2s, W2.rearrange("(c p) d -> p c d", p=P)).then_inc(back_in, 16)
            n_out = 0
            for i, blks in enumerate(HB):
                sp.wait_ge(o_ready, i + 1)
                lo, n = blks[0], len(blks)
                if blks[-1] == NBLK - 1:
                    n -= 1
                    sp.dma_start(out[(NBLK - 1) * P:N, :], otile[0:NREST, NBLK - 1, :]).then_inc(stored, 16)
                    n_out += 1
                if n:
                    sp.dma_start(out[lo * P:(lo + n) * P, :].rearrange("(i p) d -> p i d", p=P), otile[:, lo:lo + n, :]).then_inc(stored, 16)
                    n_out += 1
            sp.wait_ge(stored, 16 * n_out)

        @block.gpsimd
        def _(gp):
            def iota_to(t, pattern):
                nc.gpsimd.iota(t, pattern, base=0, channel_multiplier=0, allow_small_or_imprecise_dtypes=True).then_inc(const_ok, 1)
            nc.gpsimd.memset(ones[:, :], 1.0).then_inc(c_fill, 1)
            nc.gpsimd.memset(ones_b[:, :], 1.0)
            nc.gpsimd.memset(zero_b[:, :], 0.0)
            iota_to(zk[:, :], [[1, AB * AR * WT]])
            iota_to(iota_b[:, :], [[1, P]])
            iota_to(wbase[:, :], [[P, NBLK]])
            gp.wait_ge(c_fill, 1)
            nc.gpsimd.affine_select(out=ident[:, :], in_=ones[:, :], compare_op=ALU.is_equal, fill=0.0, base=0,
                                    pattern=[[-1, P]], channel_multiplier=1).then_inc(const_ok, 1)
            nc.gpsimd.affine_select(out=row0, in_=ones[:, :], compare_op=ALU.is_equal, fill=0.0, base=0,
                                    pattern=[[0, P]], channel_multiplier=1).then_inc(const_ok, 1)
            gp.wait_ge(h_out, 32)
            gp.wait_ge(setup_done, 1)

            def gathers(buf, b, tiles, landed):
                for k in range(tiles):
                    gp.indirect_dma_start(buf[:, k, :], None, h_rows[:, :],
                                          bass.IndirectOffsetOnAxis(ap=idx_ring[:, b, k:k + 1], axis=0)).then_inc(landed, 16)

            slow = gp.value_load(flag[0:1, 0:1], min_val=0, max_val=8 * E)
            with gp.If(slow < 1):
                def gather_step(i, u, b, kind):
                    gp.wait_ge(idx_ready, i + 1)
                    gp.sem_inc(passed["gpsimd"], 1)
                    gathers(g_gat[:, b], b, TAILG if kind == "last" else GT, gat_h[b])
                steps(gp, gather_step)
            with gp.Else():
                with gp.Fori(0, NG) as g:
                    gp.wait_ge(sl["idx"], g + 1)
                    gp.sem_inc(passed["gpsimd"], 1)
                    gathers(gbuf, 0, K, sl["gathered"])
                gp.wait_ge(sl["idx"], NG + 1)
                gathers(gbuf, 0, TT, sl["gathered"])

        @block.scalar
        def _(ac):
            ac.wait_ge(ln_stats, 1)
            nc.scalar.activation(rstd, mv[:, :, 1], ACT.Sqrt, bias=eps_c[:, :], scale=1.0).then_inc(act_sq, 1)
            ac.wait_ge(ln_scale, 1)
            for i in range(NBLK):
                last = nc.scalar.activation(hs[:, i, :], xs[:, i, :], ACT.Relu, bias=nmr[:, i:i + 1], scale=rstd[:, i:i + 1])
            last.then_inc(h_done, 1)
            ac.wait_ge(h_done, 1)
            nc.scalar.activation(hp[:, 0], hs[:, :, :], ACT.Copy).then_inc(split_done, 1)
            ac.wait_ge(split_done, 2)
            nc.scalar.activation(hp[:, 1], left[:, :, :], ACT.Copy).then_inc(split_done, 1)
            ac.wait_ge(split_done, 4)
            nc.scalar.activation(hp[:, 2], left[:, :, :], ACT.Copy).then_inc(split_done, 1)
            ac.wait_ge(setup_done, 1)
            slow = ac.value_load(flag[0:1, 0:1], min_val=0, max_val=8 * E)
            with ac.If(slow < 1):
                def count_step(i, u, b, kind):
                    ac.wait_ge(prod_done, i + 1)
                    for s in range(SETS):
                        ac.wait_ge(set_free, i * SETS + s + 3)
                        for j in range(AB):
                            n = min(AR, NBLK - j * AR)
                            last = nc.scalar.activation(cnt[:, b, j * AR:j * AR + n, s * WS:(s + 1) * WS],
                                                        set_ps[s % 2][j][:, 0:n, :], ACT.Copy)
                        last.then_inc(cnt_ready, 1)
                steps(ac, count_step)
            t = 0
            for q in range(NQ):
                for c in range(FC):
                    n = min(Q, N - q * Q)
                    ac.wait_ge(mm1, t + 1)
                    nc.scalar.activation(y1[:, c, q * Q:q * Q + n], bank[4 + t % 4][:, 0:n], ACT.Identity,
                                         bias=prm[:, c:c + 1], scale=1.0).then_inc(y_out, 1)
                    t += 1
            ac.wait_ge(bn_stat, 1)
            nc.scalar.activation(bsc[:, :, 2], bmv[:, :, 1], ACT.Sqrt, bias=eps_c[:, :], scale=1.0).then_inc(act_sq, 1)
            ac.wait_ge(bn_coef, 1)
            for q in range(NQ):
                for c in range(FC):
                    n = min(Q, N - q * Q)
                    nc.scalar.activation(y1[:, c, q * Q:q * Q + n], y1[:, c, q * Q:q * Q + n], ACT.Relu,
                                         bias=bsc[:, c, 1:2], scale=bsc[:, c, 0:1]).then_inc(y_norm, 1)
            ac.wait_ge(bn_stat, 2)
            nc.scalar.activation(bsc[:, 0:1, 2], bmv[:, 0:1, 1], ACT.Sqrt, bias=eps_c[:, :], scale=1.0).then_inc(act_sq, 1)
            ac.wait_ge(bn_coef, 2)
            for q in range(NQ):
                n = min(Q, N - q * Q)
                nc.scalar.activation(y2[:, q * Q:q * Q + n], y2[:, q * Q:q * Q + n], ACT.Relu,
                                     bias=bsc[:, 0, 1:2], scale=bsc[:, 0, 0:1]).then_inc(y_norm, 1)

        @block.vector
        def _(ve):
            n_chain = [0]

            def link(ins):
                n_chain[0] += 1
                ins.then_inc(chain, 1)
                ve.wait_ge(chain, n_chain[0])

            nc.vector.memset(xs[:, NBLK - 1, :], 0.0)
            nc.vector.memset(e_last[:, :], 0.0).then_inc(pads, 1)
            nc.vector.memset(raw_i[:, 0, NCH - 1, :], 0)
            nc.vector.memset(raw_i[:, 1, NCH - 1, :], PAD).then_inc(pads, 1)
            nc.vector.memset(eps_c[:, :], LN_EPS)
            ve.wait_ge(idx_in, 96)
            nc.vector.tensor_scalar(raw_i[:, 2], raw_i[:, 0], 7, None, ALU.logical_shift_right)
            link(nc.vector.tensor_scalar(raw_i[:, 3], raw_i[:, 0], P - 1, None, ALU.bitwise_and))
            nc.vector.tensor_copy(raw_f[:, :], raw_i[:, 1:4]).then_inc(idx_float, 1)
            ve.wait_ge(x_in, 32)
            for i in range(NBLK):
                last = nc.vector.bn_stats(stats[:, i, :], xs[:, i, :])
            link(last)
            for i in range(NBLK):
                last = nc.vector.bn_aggr(mv[:, i, :], stats[:, i, :])
            last.then_inc(ln_stats, 1)
            ve.wait_ge(act_sq, 1)
            link(nc.vector.reciprocal(rstd, rstd))
            nc.vector.scalar_tensor_tensor(out=nmr, in0=mv[:, :, 0], scalar=-1.0, in1=rstd,
                                           op0=ALU.mult, op1=ALU.mult).then_inc(ln_scale, 1)
            for n, (a, cs) in enumerate(IB):
                ve.wait_ge(idx_bank, n + 1)
                w = len(cs) * P
                last = nc.vector.tensor_copy(idxT[:, a, cs[0] * P:cs[0] * P + w], bank[4 + n % 4][:, 0:w])
                last.then_inc(idx_taken, 1)
            ve.wait_ge(firsts, 1)
            bt, relf, chk = tmp
            link(nc.vector.tensor_copy(bt, psf[:, 0:NTP]))
            link(nc.vector.tensor_tensor(relf, idxT[:, 0], bt, ALU.subtract))
            nc.vector.tensor_copy(rel[:, :], relf)
            nc.vector.tensor_copy(row[:, :], idxT[:, 2])
            nc.vector.scalar_tensor_tensor(out=key[:, :], in0=idxT[:, 1], scalar=float(WT), in1=relf, op0=ALU.mult, op1=ALU.add)
            link(nc.vector.scalar_tensor_tensor(out=idxT[:, 1], in0=idxT[:, 1], scalar=float(P), in1=idxT[:, 2], op0=ALU.mult, op1=ALU.add))
            nc.vector.tensor_copy(gat_src[:, :, :], idxT[:, 1, 0:(NSTEP + 1) * T].rearrange("p (i t) -> p i t", t=T)[:, :, CT:T]).then_inc(tables_ok, 1)
            chk1 = chk[:, 0:NT]
            link(nc.vector.tensor_scalar(chk1, relf[:, 0:NT], float(WT), None, ALU.is_ge))
            link(nc.vector.scalar_tensor_tensor(out=chk1, in0=relf[:, 0:NT], scalar=PAD / 2.0, in1=chk1, op0=ALU.is_lt, op1=ALU.mult))
            link(nc.vector.scalar_tensor_tensor(out=chk1, in0=relf[:, 0:NT], scalar=0.0, in1=chk1, op0=ALU.is_lt, op1=ALU.add))
            link(nc.vector.tensor_reduce(viol[:, 0:1], chk1, axis=AX.X, op=ALU.add))
            TI = (NSTEP + 1) * T
            btv = bt[:, 0:TI].rearrange("p (i t) -> p i t", t=T)
            offv = relf[:, 0:TI].rearrange("p (i t) -> p i t", t=T)
            chkv = chk[:, 0:TI].rearrange("p (i t) -> p i t", t=T)
            for s in range(SETS):
                nc.vector.tensor_tensor(offv[:, :, s * ST:(s + 1) * ST], btv[:, :, s * ST:(s + 1) * ST],
                                        btv[:, :, s * ST:s * ST + 1].to_broadcast([P, NSTEP + 1, ST]), ALU.subtract)
            link(nc.vector.tensor_tensor(offv[:, :, CT:T], btv[:, :, CT:T], btv[:, :, CT:CT + 1].to_broadcast([P, NSTEP + 1, GT]), ALU.subtract))
            nc.vector.tensor_copy(base_i[:, :].rearrange("p (i s) -> p i s", s=NBASE), btv[:, :, 0:CT + 1:ST])
            nc.vector.tensor_copy(off_i[:, 0:TI], relf[:, 0:TI])
            link(nc.vector.tensor_scalar(chkv[:, :, 0:CT], offv[:, :, 0:CT], float(WS - WT), None, ALU.is_gt))
            link(nc.vector.tensor_reduce(viol[:, 1:2], chkv[:, :, 0:CT], axis=AX.XY, op=ALU.add))
            link(nc.vector.memset(chk, 0.0))
            link(nc.vector.tensor_scalar(chkv[:, 0:NSTEP, CT:T], offv[:, 0:NSTEP, CT:T], float(WG - WT), None, ALU.is_gt))
            link(nc.vector.tensor_scalar(chkv[:, NSTEP:NSTEP + 1, CT:CT + TAILG], offv[:, NSTEP:NSTEP + 1, CT:CT + TAILG], float(WG - WT), None, ALU.is_gt))
            link(nc.vector.tensor_reduce(viol[:, 2:3], chk, axis=AX.X, op=ALU.add))
            link(nc.vector.tensor_scalar(chk[:, 0:NT], relf[:, 0:NT], 0.0, None, ALU.is_lt))
            link(nc.vector.tensor_reduce(viol[:, 3:4], chk[:, 0:NT], axis=AX.X, op=ALU.add))
            link(nc.vector.memset(chk, 0.0))
            for s in range(SETS):
                link(nc.vector.tensor_tensor(chkv[:, :, s * ST + 1:(s + 1) * ST], offv[:, :, s * ST + 1:(s + 1) * ST],
                                             offv[:, :, s * ST:(s + 1) * ST - 1], ALU.subtract))
            link(nc.vector.tensor_scalar(chk, chk, float(WT), None, ALU.is_gt))
            link(nc.vector.tensor_reduce(viol[:, 4:5], chk, axis=AX.X, op=ALU.add))
            lastv = offv[:, :, ST - 1:CT:ST]
            link(nc.vector.tensor_scalar(chkv[:, :, 0:SETS], lastv, float(COVER - WT), None, ALU.is_lt))
            link(nc.vector.tensor_reduce(viol[:, 5:6], chkv[:, :, 0:SETS], axis=AX.XY, op=ALU.add))
            nc.vector.tensor_reduce(viol[:, 6:7], viol[:, 0:6], axis=AX.X, op=ALU.add).then_inc(viol_ok, 1)
            ve.wait_ge(split_done, 1)
            nc.vector.tensor_tensor(left[:, :, :], hs[:, :, :], hp[:, 0], ALU.subtract).then_inc(split_done, 1)
            ve.wait_ge(split_done, 3)
            nc.vector.tensor_tensor(left[:, :, :], left[:, :, :], hp[:, 1], ALU.subtract).then_inc(split_done, 1)
            ve.wait_ge(tables_out, 16)
            link(nc.vector.memset(acc[:, :, :], 0.0))
            ve.wait_ge(viol_sum, 1)
            link(nc.vector.tensor_copy(flag[:, :], bank[4][:, 0:1]))
            ve.wait_ge(const_ok, 5)
            ve.wait_ge(split_done, 5)
            ve.sem_inc(setup_done, 1)

            slow = ve.value_load(flag[0:1, 0:1], min_val=0, max_val=8 * E)
            with ve.If(slow < 1):
                for s_, credit in ((set_free, 2), (cnt_ready, 2), (ring_free, RING), (step_summed, 2), (prod_done, 2),
                                   (prod_taken, 1), (ed_taken, 1), (acc_add, 1)):
                    ve.sem_inc(s_, credit)
                nc.vector.tensor_copy(idx_ring[:, 0, :], gat_src[:, 0, :]).then_inc(idx_ready, 1)
                ADDS = NBASE + SETS

                def bases(i, n):
                    return nc.values_load_multi_w_load_instructions(base_i[0:1, bass.ds(i * NBASE, n)], engines=(DVE_ENGINE,),
                                                                    min_val=0, max_val=N - 1)[1]

                def add_edges(i):
                    base = bases(i, NBASE)
                    ve.wait_ge(step_summed, i + 3)
                    for s in range(NBASE):
                        w = WS if s < SETS else WG
                        a = acc[:, :, bass.ds(base[s], w)]
                        ve.wait_ge(acc_add, i * ADDS + s + 1)
                        nc.vector.tensor_tensor(a, a, ed[:, :, s * WS:s * WS + w], ALU.add).then_inc(acc_add, 1)
                    ve.wait_ge(acc_add, i * ADDS + NBASE + 1)
                    nc.vector.memset(ed[:, :, 0:SETS * WS + WG], 0.0).then_inc(ed_taken, 1)

                def add_products(i):
                    base = bases(i, SETS)
                    ve.wait_ge(prod_done, i + 3)
                    for s in range(SETS):
                        a = acc[:, 0, bass.ds(base[s], WS)]
                        ve.wait_ge(acc_add, i * ADDS + NBASE + s + 1)
                        nc.vector.tensor_tensor(a, a, prod[:, s * WS:(s + 1) * WS], ALU.add).then_inc(acc_add, 1)
                    ve.wait_ge(acc_add, i * ADDS + ADDS + 1)
                    nc.vector.memset(prod, 0.0).then_inc(prod_taken, 1)

                def hots(i, s):
                    ve.wait_ge(set_free, i * SETS + s + 1)
                    for k in range(ST):
                        t = i * T + (s * ST + k)
                        nc.vector.tensor_scalar(zhot[:, s % 2, k, :], zk[:, :], key[:, bass.ds(t, 1)], None, ALU.is_equal)
                        last = nc.vector.tensor_scalar(rhot[:, s % 2, k, :], iota_b[:, :], row[:, bass.ds(t, 1)], None, ALU.is_equal)
                    last.then_inc(hot_ready, 1)

                def one_step(i, u, b, kind):
                    g = TAILG if kind == "last" else GT
                    ve.wait_ge(step_summed, i + 1)
                    for t in (dhot, dhot_b):
                        last = nc.vector.tensor_tensor(t[:, b, 0:CT + g, :], iota_b[:, 0:WT].unsqueeze(1).to_broadcast([P, CT + g, WT]),
                                                       rel[:, bass.ds(i * T, CT + g)].unsqueeze(2).to_broadcast([P, CT + g, WT]), ALU.is_equal)
                    last.then_inc(dhot_ready, 1)
                    hots(i, 0)
                    hots(i, 1)
                    if kind != "first":
                        add_edges(i - 1)
                    if kind != "last":
                        ve.wait_ge(step_summed, i + 2)
                        nc.vector.tensor_copy(idx_ring[:, 1 - b, :], gat_flat[:, bass.ds(i * GT + GT, GT)]).then_inc(idx_ready, 1)
                    hots(i, 2)
                    if kind != "first":
                        add_products(i - 1)
                    hots(i, 3)
                    hots(i, 4)
                    if kind == "last":
                        ve.wait_ge(gat_e[b], u * 32 + 16)
                        ve.wait_ge(gat_h[b], u * (16 * GT) + 16 * TAILG)
                        ve.wait_ge(last_edges, 16)
                        nc.vector.tensor_tensor(e_gat[:, b, 0:g - 1, :], e_gat[:, b, 0:g - 1, :], g_gat[:, b, 0:g - 1, :], ALU.add)
                        nc.vector.tensor_tensor(e_last[:, :], e_last[:, :], g_gat[:, b, g - 1, :], ALU.add).then_inc(gat_ready, 1)
                    else:
                        ve.wait_ge(gat_e[b], u * 32 + 32)
                        ve.wait_ge(gat_h[b], u * (16 * GT) + 16 * GT)
                        nc.vector.tensor_tensor(e_gat[:, b], e_gat[:, b], g_gat[:, b], ALU.add).then_inc(gat_ready, 1)
                    hots(i, 5)
                steps(ve, one_step)
                add_edges(NSTEP)
                add_products(NSTEP)
                ve.wait_ge(acc_add, (NSTEP + 1) * ADDS + 1)
                ve.sem_inc(sums_done, 1)
            with ve.Else():
                ve.wait_ge(tables_in, 16)
                ve.sem_inc(sl["added"], 1)

                def window(g, w, tiles, dests):
                    nth = g * NBLK + w
                    nc.vector.tensor_copy(rel_w[:, 0:tiles], dests).then_inc(sl["step"], 1)
                    ve.wait_ge(sl["step"], nth * 2 + 1)
                    nc.vector.tensor_tensor(rel_w[:, 0:tiles], rel_w[:, 0:tiles], wbase[:, bass.ds(w, 1)].to_broadcast([P, tiles]),
                                            ALU.subtract).then_inc(sl["step"], 1)
                    ve.wait_ge(sl["step"], nth * 2 + 2)
                    nc.vector.tensor_tensor(onehot[:, 0:tiles, :], iota_b[:, :].unsqueeze(1).to_broadcast([P, tiles, P]),
                                            rel_w[:, 0:tiles].unsqueeze(2).to_broadcast([P, tiles, P]), ALU.is_equal).then_inc(sl["onehot"], 1)
                    ve.wait_ge(sl["mm"], nth + 1)
                    for j in range(2):
                        a = acc[:, j, bass.ds(w * P, P)]
                        last = nc.vector.tensor_tensor(a, a, bank[6 + j][:, 0:P], ALU.add)
                    return last

                with ve.Fori(0, NG) as g:
                    nc.vector.tensor_copy(idx_ring[:, 0, 0:K], sd[:, 1, bass.ds(g * K, K)]).then_inc(sl["idx"], 1)
                    with ve.Fori(0, NBLK) as w:
                        window(g, w, K, sd[:, 0, bass.ds(g * K, K)]).then_inc(sl["added"], 1)
                        ve.wait_ge(sl["added"], g * NBLK + w + 2)
                nc.vector.memset(ebuf[:, TT - 1, :], 0.0).then_inc(sl["added"], 1)
                nc.vector.tensor_copy(idx_ring[:, 0, 0:TT], sd[:, 1, NG * K:NT]).then_inc(sl["idx"], 1)
                with ve.Fori(0, NBLK) as w:
                    window(NG, w, TT, sd[:, 0, NG * K:NT]).then_inc(sl["tail"], 1)
                    ve.wait_ge(sl["tail"], w + 1)
                ve.sem_inc(sums_done, 1)

            ve.wait_ge(prm_in, 112)
            link(nc.vector.tensor_scalar(acc[:, 1, 0:N], acc[:, 1, 0:N], 1.0, None, ALU.max))
            link(nc.vector.reciprocal(acc[:, 1, 0:N], acc[:, 1, 0:N]))
            link(nc.vector.tensor_tensor(acc[:, 0, 0:N], acc[:, 0, 0:N], acc[:, 1, 0:N], ALU.mult))
            link(nc.vector.tensor_scalar(epsb[:, :], epsb[:, :], 1.0, None, ALU.add))

            def stat_chunk(q):
                n = min(Q, N - q * Q)
                for c in range(FC):
                    ve.wait_ge(y_out, q * FC + c + 1)
                    last = nc.vector.bn_stats(bstat[:, c, q, :], y1[:, c, q * Q:q * Q + n])
                return last

            for q in range(NQ):
                n = min(Q, N - q * Q)
                ve.wait_ge(zT, q + 1)
                nc.vector.scalar_tensor_tensor(out=acc[:, 0, q * Q:q * Q + n], in0=bank[q % 4][:, 0:n], scalar=epsb[:, :],
                                               in1=acc[:, 0, q * Q:q * Q + n], op0=ALU.mult, op1=ALU.add).then_inc(z_ready, 1)
                if q >= 2:
                    stat_chunk(q - 2)
            stat_chunk(NQ - 2)
            last = stat_chunk(NQ - 1)

            def scale_shift(last, nch, pg, pb, sq):
                link(last)
                for cc in range(nch):
                    last = nc.vector.bn_aggr(bmv[:, cc, :], bstat[:, cc, :, :].rearrange("p q s -> p (q s)"))
                last.then_inc(bn_stat, 1)
                ve.wait_ge(act_sq, sq)
                link(nc.vector.reciprocal(bsc[:, 0:nch, 2], bsc[:, 0:nch, 2]))
                link(nc.vector.tensor_tensor(bsc[:, 0:nch, 0], prm[:, pg:pg + nch], bsc[:, 0:nch, 2], ALU.mult))
                link(nc.vector.tensor_tensor(bsc[:, 0:nch, 1], bmv[:, 0:nch, 0], bsc[:, 0:nch, 0], ALU.mult))
                nc.vector.tensor_tensor(bsc[:, 0:nch, 1], prm[:, pb:pb + nch], bsc[:, 0:nch, 1], ALU.subtract).then_inc(bn_coef, 1)

            scale_shift(last, FC, FC, 2 * FC, 2)
            for q in range(NQ):
                n = min(Q, N - q * Q)
                ve.wait_ge(mm2, q + 1)
                nc.vector.tensor_scalar(y2[:, q * Q:q * Q + n], bank[q % 8][:, 0:n], prm[:, 3 * FC:3 * FC + 1], None, ALU.add).then_inc(y2_out, 1)
                ve.wait_ge(y2_out, q + 1)
                last = nc.vector.bn_stats(bstat[:, 0, q, :], y2[:, q * Q:q * Q + n])
            scale_shift(last, 1, 3 * FC + 1, 3 * FC + 2, 3)
            ve.wait_ge(back_in, 96)
            for i, blks in enumerate(HB):
                ve.wait_ge(o_T, i + 1)
                w = len(blks) * P
                lo = blks[0]
                rows = NREST if blks == [NBLK - 1] else P
                nc.vector.tensor_tensor(otile[0:rows, lo:lo + len(blks), :], xback[0:rows, lo:lo + len(blks), :],
                                        bank[i % 8][0:rows, 0:w].rearrange("p (i d) -> p i d", d=D), ALU.add).then_inc(o_ready, 1)

        @block.tensor
        def _(te):
            te.wait_ge(const_ok, 5)
            te.wait_ge(idx_float, 1)
            for n, (a, cs) in enumerate(IB):
                if n >= 4:
                    te.wait_ge(idx_taken, n - 3)
                for j, c in enumerate(cs):
                    last = nc.tensor.transpose(bank[4 + n % 4][:, j * P:(j + 1) * P], raw_f[:, a, c, :], ident[:, :])
                last.then_inc(idx_bank, 1)
            te.wait_ge(idx_taken, len(IB))
            for q in range(0, NTP, Q):
                n = min(Q, NTP - q)
                last = nc.tensor.matmul(psf[:, q:q + n], row0, idxT[:, 0, q:q + n], start=True, stop=True)
            last.then_inc(firsts, 1)
            te.wait_ge(viol_ok, 1)
            nc.tensor.matmul(bank[4][:, 0:1], ones[:, :], viol[:, 6:7], start=True, stop=True).then_inc(viol_sum, 1)
            te.wait_ge(setup_done, 1)
            slow = te.value_load(flag[0:1, 0:1], min_val=0, max_val=8 * E)
            with te.If(slow < 1):
                for j in (6, 7):
                    for h in range(2):
                        nc.tensor.matmul(bank[j][:, h * Q // 2:(h + 1) * Q // 2], zero_b[:, :], zk[:, 0:Q // 2], start=(h == 0), stop=True,
                                         skip_group_check=True)

                def places(t, n, most):
                    return nc.values_load_multi_w_load_instructions(off_i[0:1, bass.ds(t, n)], engines=(PE_ENGINE,),
                                                                    min_val=0, max_val=most - WT,
                                                                    skip_runtime_bounds_check_because="the flag says that all places fit")[1]

                def count(i, u, b, s):
                    offs = places(i * T + s * ST, ST, WS)
                    te.wait_ge(cnt_ready, i * SETS + s + 1)
                    te.wait_ge(hot_ready, i * SETS + s + 1)
                    for j in range(AB):
                        nc.tensor.matmul(set_ps[s % 2][j][:, :, COVER:WS], zero_b[:, :],
                                         zk[:, 0:AR * (WS - COVER)].rearrange("p (a w) -> p a w", a=AR),
                                         start=True, stop=False, skip_group_check=True)
                    for k in range(ST):
                        for j in range(AB):
                            o = set_ps[s % 2][j]
                            o = o[:, :, 0:WT] if k == 0 else o[:, :, bass.ds(offs[k], WT)]
                            last = nc.tensor.matmul(o, rhot[:, s % 2, k, :],
                                                    zhot[:, s % 2, k, j * AR * WT:(j + 1) * AR * WT].rearrange("p (a w) -> p a w", a=AR),
                                                    start=False, stop=(k == ST - 1), skip_group_check=True)
                    last.then_inc(set_free, 1)
                    return offs

                def sum_tile(col, edges, b, t):
                    nc.tensor.matmul(ed[:, 0, bass.ds(col, WT)], edges, dhot[:, b, t, :], start=False, stop=True, skip_group_check=True)
                    return nc.tensor.matmul(ed[:, 1, bass.ds(col, WT)], ones_b[:, :], dhot_b[:, b, t, :], start=False, stop=True,
                                            skip_group_check=True)

                def sum_set(i, u, b, s, offs):
                    r = (SETS * b + s) % RING
                    te.wait_ge(cnt_landed[r], u * (16 * 2 * SETS // RING) + ((SETS * b + s) // RING + 1) * 16)
                    for k in range(ST):
                        last = sum_tile(offs[k] + s * WS if k else s * WS, e_cnt[:, r, k, :], b, s * ST + k)
                    last.then_inc(ring_free, 1)

                def product(i, b):
                    te.wait_ge(cnt_ready, i * SETS + (SETS + 2))
                    te.wait_ge(prod_taken, i + 1)
                    for a in range(NBLK):
                        for p_ in range(3):
                            last = nc.tensor.matmul(prod, hp[:, p_, a, :], cnt[:, b, a, :], start=False, stop=True, skip_group_check=True)
                    last.then_inc(prod_done, 1)

                def pe_step(i, u, b, kind):
                    offs = count(i, u, b, 0)
                    if kind != "first":
                        product(i - 1, 1 - b)
                    te.wait_ge(ed_taken, i + 1)
                    te.wait_ge(dhot_ready, i + 1)
                    sum_set(i, u, b, 0, offs)
                    for s in range(1, SETS):
                        offs = count(i, u, b, s)
                        sum_set(i, u, b, s, offs)
                    g = TAILG if kind == "last" else GT
                    te.wait_ge(gat_ready, i + 1)
                    for k0 in range(0, g, 5):
                        offs = places(i * T + CT + k0, min(5, g - k0), WG)
                        for k in range(k0, min(k0 + 5, g)):
                            edges = e_last[:, :] if kind == "last" and k == g - 1 else e_gat[:, b, k, :]
                            last = sum_tile(offs[k - k0] + SETS * WS, edges, b, CT + k)
                    last.then_inc(step_summed, 1)
                steps(te, pe_step)
                product(NSTEP, 0)
            with te.Else():
                def group(tiles):
                    for k in range(tiles):
                        nc.tensor.matmul(bank[6][:, 0:P], ebuf[:, k, :], onehot[:, k, :], start=(k == 0), stop=False)
                        nc.tensor.matmul(bank[6][:, 0:P], gbuf[:, k, :], onehot[:, k, :], start=False, stop=(k == tiles - 1))
                        last = nc.tensor.matmul(bank[7][:, 0:P], ones[:, :], onehot[:, k, :], start=(k == 0), stop=(k == tiles - 1))
                    return last
                with te.Fori(0, NG) as g:
                    te.wait_ge(sl["loaded"], g * 32 + 32)
                    te.wait_ge(sl["gathered"], g * (16 * K) + 16 * K)
                    te.sem_inc(passed["tensor"], 1)
                    with te.Fori(0, NBLK) as w:
                        te.wait_ge(sl["onehot"], g * NBLK + w + 1)
                        group(K).then_inc(sl["mm"], 1)
                te.wait_ge(sl["loaded"], NG * 32 + 32)
                te.wait_ge(sl["gathered"], NG * 16 * K + 16 * TT)
                with te.Fori(0, NBLK) as w:
                    te.wait_ge(sl["onehot"], w + (NG * NBLK + 1))
                    group(TT).then_inc(sl["mm"], 1)

            def layer1(q):
                te.wait_ge(z_ready, q + 1)
                n = min(Q, N - q * Q)
                for c in range(FC):
                    t = q * FC + c
                    if t >= 4:
                        te.wait_ge(y_out, t - 3)
                    nc.tensor.matmul(bank[4 + t % 4][:, 0:n], w1s[:, c * P:(c + 1) * P], acc[:, 0, q * Q:q * Q + n],
                                     start=True, stop=True).then_inc(mm1, 1)

            te.wait_ge(back_in, 96)
            for q in range(NQ):
                if q >= 4:
                    te.wait_ge(z_ready, q - 3)
                for j, c in enumerate(HB[q]):
                    w = min(P, N - c * P)
                    last = nc.tensor.transpose(bank[q % 4][:, j * P:j * P + w], hback[0:w, c, :], ident[0:w, 0:w])
                last.then_inc(zT, 1)
                if q:
                    layer1(q - 1)
            layer1(NQ - 1)
            te.wait_ge(y_out, NQ * FC)
            for q in range(NQ):
                n = min(Q, N - q * Q)
                te.wait_ge(y_norm, (q + 1) * FC)
                if q >= 8:
                    te.wait_ge(y2_out, q - 7)
                for c in range(FC):
                    last = nc.tensor.matmul(bank[q % 8][:, 0:n], w2s[:, c, :], y1[:, c, q * Q:q * Q + n],
                                            start=(c == 0), stop=(c == FC - 1))
                last.then_inc(mm2, 1)
            te.wait_ge(y2_out, NQ)
            for i, blks in enumerate(HB):
                te.wait_ge(y_norm, NQ * FC + i + 1)
                if i >= 8:
                    te.wait_ge(o_ready, i - 7)
                for j, c in enumerate(blks):
                    w = min(P, N - c * P)
                    last = nc.tensor.transpose(bank[i % 8][0:w, j * P:(j + 1) * P], y2[:, c * P:c * P + w], ident[:, :])
                last.then_inc(o_T, 1)


_INS = ['x', 'src', 'dst', 'edge_attr_128', 'L0_gnn_eps', 'L0_gnn_W1', 'L0_gnn_b1', 'L0_gnn_gamma1', 'L0_gnn_beta1',
        'L0_gnn_W2', 'L0_gnn_b2', 'L0_gnn_gamma2', 'L0_gnn_beta2']


def kernel(**inputs):
    import numpy as _np
    import concourse.bacc as _bacc
    from concourse import mybir as _mybir
    from concourse.bass_utils import run_bass_kernel_spmd as _run

    nc = _bacc.Bacc("TRN2", target_bir_lowering=False, num_devices=1)
    arrays, args = {}, []
    for name in _INS:
        a = _np.ascontiguousarray(inputs[name])
        arrays[f"in_{name}"] = a
        args.append(nc.dram_tensor(f"in_{name}", a.shape, _mybir.dt.from_np(a.dtype), kind="ExternalInput").ap())
    shape = inputs['x'].shape
    args.append(nc.dram_tensor("out_x", shape, _mybir.dt.float32, kind="ExternalOutput").ap())
    args.append(nc.dram_tensor("h_rows", shape, _mybir.dt.float32, kind="Internal").ap())
    n_tables = 2 * (-(-inputs['src'].shape[0] // 128 ** 2)) * 128
    args.append(nc.dram_tensor("tables", (128, n_tables), _mybir.dt.float32, kind="Internal").ap())
    gnn_layer(nc, *args)
    r = _run(nc, [arrays], core_ids=[0])
    return r.results[0]["out_x"]
```

```python
import concourse.bass as bass
from concourse import mybir
from contextlib import ExitStack

F32 = mybir.dt.float32
I32 = mybir.dt.int32
I16 = mybir.dt.int16
F16 = mybir.dt.float16
BF16 = mybir.dt.bfloat16
ALU = mybir.AluOpType
ACT = mybir.ActivationFunctionType
AX = mybir.AxisListType
PE_ENGINE = mybir.EngineType.PE
DVE_ENGINE = mybir.EngineType.DVE


def gnn_layer(nc, x, src, dst, edge, eps, W1, b1, gamma1, beta1, W2, b2, gamma2, beta2, out, h_rows, tables):
    P = 128
    N, D = x.shape
    E = src.shape[0]
    F = W1.shape[1]
    FC = F // P
    NBLK = -(-N // P)
    NREST = N - (NBLK - 1) * P
    NT = -(-E // P)
    TREST = E - (NT - 1) * P
    NCH = -(-NT // P)
    NTP = NCH * P
    CROW = NT - 1 - (NCH - 1) * P
    PAD = 30000

    SETS, ST, GT = 5, 6, 22
    CT = SETS * ST
    T = CT + GT
    NSTEP = (NT - 1) // T
    TAILG = NT - NSTEP * T - CT
    assert NSTEP % 2 == 0 and 0 < TAILG <= GT
    WT = 7
    WS = 30
    WG = 100
    COVER = 21
    AB = 3
    AR = -(-NBLK // AB)
    RING = 5
    WC = SETS * WS
    NBASE = SETS + 1
    DRING = 5
    PER_COUNT, PER_SUM, PER_GATHERED = (3, 4), 1, 1

    K = 16
    NG = NT // K
    TT = NT - NG * K

    NACC = max(N + 100, NBLK * P)
    Q = 512
    NQ = -(-N // Q)
    CH = 3 * P
    DONE = (NSTEP // 2 - 1) * CH
    assert 0 < DONE < N
    LN_EPS = 1e-5

    ctx = ExitStack()
    with ctx:
        def sb(name, shape, dt=F32):
            return ctx.enter_context(nc.sbuf_tensor(name, shape, dt))

        def sem(name):
            return ctx.enter_context(nc.semaphore(name))

        ZW = AB * AR * WT + (AB * AR * WT) % 2
        sizes = [RING * ST * D, 2 * GT * D, 2 * NBLK * WC // 2, 2 * ST * ZW // 2]
        at = [sum(sizes[:i]) for i in range(len(sizes) + 1)]
        BD = NBLK * D
        before = 3 * BD + 6 * NBLK + P + 4 * NBLK
        after = max(FC * NQ * Q + BD, before) + 2 * F + FC * NQ * 6
        assert max(at[-1], before) <= FC * NQ * Q + BD
        stage = sb("stage", [P, max(at[-1], before, after)])
        e_cnt = stage[:, at[0]:at[1]].rearrange("p (r k d) -> p r k d", r=RING, k=ST)
        e_gat = stage[:, at[1]:at[2]].rearrange("p (b k d) -> p b k d", b=2, k=GT)
        cnt = stage[:, at[2]:at[3]].bitcast(F16).rearrange("p (b a w) -> p b a w", b=2, a=NBLK)
        zhot = stage[:, at[3]:at[4]].bitcast(F16).rearrange("p (b k w) -> p b k w", b=2, k=ST)
        xs = stage[:, 0:BD].rearrange("p (i d) -> p i d", d=D)
        hs = stage[:, BD:2 * BD].rearrange("p (i d) -> p i d", d=D)
        left = stage[:, 2 * BD:3 * BD].rearrange("p (i d) -> p i d", d=D)
        stats = stage[:, 3 * BD:3 * BD + 6 * NBLK].rearrange("p (i s) -> p i s", s=6)
        row0 = stage[:, 3 * BD + 6 * NBLK:3 * BD + 6 * NBLK + P]
        LN = 3 * BD + 6 * NBLK + P
        mv = stage[:, LN:LN + 2 * NBLK].rearrange("p (i s) -> p i s", s=2)
        rstd = stage[:, LN + 2 * NBLK:LN + 3 * NBLK]
        nmr = stage[:, LN + 3 * NBLK:LN + 4 * NBLK]
        y1 = stage[:, 0:FC * NQ * Q].rearrange("p (c n) -> p c n", c=FC)
        xback = stage[:, FC * NQ * Q:FC * NQ * Q + BD].rearrange("p (i d) -> p i d", d=D)
        AFTER = max(FC * NQ * Q + BD, before)
        w1s = stage[:, AFTER:AFTER + F]
        w2s = stage[:, AFTER + F:AFTER + F + FC * D].rearrange("p (c d) -> p c d", c=FC)
        bstat = stage[:, AFTER + 2 * F:AFTER + 2 * F + FC * NQ * 6].rearrange("p (c q s) -> p c q s", c=FC, q=NQ)
        ebuf = stage[:, at[1]:at[1] + K * D].rearrange("p (k d) -> p k d", k=K)
        gbuf = stage[:, at[1] + K * D:at[1] + 2 * K * D].rearrange("p (k d) -> p k d", k=K)
        onehot = stage[:, at[2]:at[2] + K * P].rearrange("p (k w) -> p k w", k=K)
        rel_w = stage[:, at[3]:at[3] + K]
        sd = stage[:, at[2] + K * P:at[2] + K * P + 2 * NTP].rearrange("p (a t) -> p a t", a=2)

        acc = sb("acc", [P, 2, NACC])
        accf = acc[:, :, :].rearrange("p a n -> p (a n)")
        raw_i = accf[:, 0:4 * NTP].bitcast(I32).rearrange("p (a c e) -> p a c e", a=4, c=NCH)
        raw_f = accf[:, NTP:4 * NTP].rearrange("p (a c e) -> p a c e", a=3, c=NCH)
        idxT = accf[:, 4 * NTP:7 * NTP].rearrange("p (a t) -> p a t", a=3)
        tmp = [accf[:, j * NTP:(j + 1) * NTP] for j in range(3)]
        y2 = acc[:, 1, :]
        otile = acc[:, 0, 0:NBLK * P].rearrange("p (i d) -> p i d", d=D)
        hp = sb("hp", [P, 3, NBLK, D], BF16)


        key = sb("key", [P, NTP], F16)
        row = sb("row", [P, NTP], F16)
        rel = sb("rel", [P, NTP], BF16)
        gat_src = sb("gat_src", [P, NSTEP + 1, GT], I16)
        gat_flat = gat_src[:, :, :].rearrange("p i g -> p (i g)")
        off_i = sb("off_i", [P, (NSTEP + 1) * CT], I32)
        base_i = sb("base_i", [P, (NSTEP + 1) * NBASE], I32)
        idx_ring = sb("idx_ring", [P, 2, GT], I32)
        rhot = sb("rhot", [P, 2, ST, P], F16)
        dhot = sb("dhot", [P, DRING, ST, WS])
        dhot_b = sb("dhot_b", [P, DRING, ST, WS], BF16)
        ghot = sb("ghot", [P, GT, WG])
        ghot_b = sb("ghot_b", [P, GT, WG], BF16)
        e_last = sb("e_last", [P, D])

        zk = sb("zk", [P, ZW], F16)
        iota_b = sb("iota_b", [P, P], BF16)
        ident_b = sb("ident_b", [P, P], BF16)
        ident = sb("ident", [P, P])
        ones = sb("ones", [P, P])
        ones_b = sb("ones_b", [P, P], BF16)
        zero_b = sb("zero_b", [P, P], BF16)
        wbase = sb("wbase", [P, NBLK])
        eps_c = sb("eps_c", [P, 1])
        viol = sb("viol", [P, 11])
        ext = sb("ext", [P, 8])
        ahead = sb("ahead", [P, NSTEP // 2 - 1])
        flag = sb("flag", [P, 1], I32)
        prm = sb("prm", [P, 9])
        epsb = sb("epsb", [P, 1])
        bmv = sb("bmv", [P, FC, 2])
        bsc = sb("bsc", [P, FC, 3])
        ps = ctx.enter_context(nc.psum_tensor("ps", [P, 8, Q], F32))
        bank = [ps[:, i, :] for i in range(8)]
        set_ps = [[bank[AB * b + j][:, 0:AR * WS].rearrange("p (a w) -> p a w", a=AR) for j in range(AB)] for b in range(2)]
        sums = [bank[6 + b].rearrange("p (a n) -> p a n", a=2) for b in range(2)]
        last_prod = bank[4][:, 0:WC]
        psf = ps[:, :, :].rearrange("p b n -> p (b n)")

        XC = [(NBLK * c // 4, NBLK * (c + 1) // 4) for c in range(4)]
        x_in = [sem(f"x_in{c}") for c in range(len(XC))]
        idx_in, prm_in = sem("idx_in"), sem("prm_in")
        c_fill, const_ok, pads = sem("c_fill"), sem("const_ok"), sem("pads")
        ln_stats, ln_scale, h_done = sem("ln_stats"), sem("ln_scale"), sem("h_done")
        act_sq, h_out = sem("act_sq"), sem("h_out")
        part_done = sem("part_done")
        left_done = sem("left_done")
        acc_zero = sem("acc_zero")
        idx_float, idx_bank, idx_taken = sem("idx_float"), sem("idx_bank"), sem("idx_taken")
        firsts, viol_ok, viol_sum = sem("firsts"), sem("viol_ok"), sem("viol_sum")
        tables_ok, tables_out, tables_in = sem("tables_ok"), sem("tables_out"), sem("tables_in")
        setup_done, last_edges = sem("setup_done"), sem("last_edges")
        chain = sem("chain")
        passed = {n: sem("passed_" + n) for n in ("sync", "gpsimd", "tensor", "vector")}

        set_free = sem("set_free")
        hot_ready = sem("hot_ready")
        cnt_ready = sem("cnt_ready")
        ring_free = sem("ring_free")
        cnt_landed = [sem(f"cnt_landed{r}") for r in range(RING)]
        step_summed = sem("step_summed")
        dcopy_ready = sem("dcopy_ready")
        ghot_ready = sem("ghot_ready")
        gcopy_ready = sem("gcopy_ready")
        idx_ready = sem("idx_ready")
        gat_e = [sem(f"gat_e{b}") for b in range(2)]
        gat_h = [sem(f"gat_h{b}") for b in range(2)]
        prod_done = sem("prod_done")
        sums_taken = sem("sums_taken")
        acc_add = sem("acc_add")
        inverted = sem("inverted")
        sums_done = sem("sums_done")

        sl = {n: sem("slow_" + n) for n in ("loaded", "gathered", "idx", "onehot", "mm", "added", "tail", "step")}

        w_in, back_in, zT, z_ready = sem("w_in"), sem("back_in"), sem("zT"), sem("z_ready")
        mean_ok = sem("mean_ok")
        mm1, y_out, y_stat = sem("mm1"), sem("y_out"), sem("y_stat")
        bn_stat, bn_coef, y_norm = sem("bn_stat"), sem("bn_coef"), sem("y_norm")
        mm2, y2_out, o_T, o_ready, stored = sem("mm2"), sem("y2_out"), sem("o_T"), sem("o_ready"), sem("stored")

        block = ctx.enter_context(nc.Block())

        TPB = Q // P
        HB = [list(range(i, min(i + TPB, NBLK))) for i in range(0, NBLK, TPB)]
        IB = [(a, list(range(i, min(i + TPB, NCH)))) for a in range(3) for i in range(0, NCH, TPB)]

        def steps(eng, body):
            for i in range(2):
                body(i, 0, i, ("first", "second")[i])
            with eng.Fori(1, NSTEP // 2) as u:
                for b in range(2):
                    body(u * 2 + b, u, b, "whole")
            body(NSTEP, NSTEP // 2, 0, "last")

        def gathered(b, k, kind):
            return e_last[:, :] if kind == "last" and k == TAILG - 1 else e_gat[:, b, k, :]

        @block.sync
        def _(sp):
            sp.wait_ge(pads, 2)
            for a, v in enumerate((src, dst)):
                full = (NCH - 1) * P * P
                sp.dma_start(raw_i[:, a, 0:NCH - 1, :], v[0:full].rearrange("(c p e) -> p c e", p=P, e=P)).then_inc(idx_in, 16)
                sp.dma_start(raw_i[0:CROW, a, NCH - 1, :], v[full:full + CROW * P].rearrange("(p e) -> p e", e=P)).then_inc(idx_in, 16)
                sp.dma_start(raw_i[CROW:CROW + 1, a, NCH - 1, 0:TREST], v[E - TREST:E].rearrange("(p e) -> p e", p=1)).then_inc(idx_in, 16)
            sp.dma_start(e_last[0:TREST, :], edge[E - TREST:E, :]).then_inc(last_edges, 16)
            sp.dma_start(w1s, W1).then_inc(w_in, 16)
            sp.dma_start(w2s, W2.rearrange("(c p) d -> p c d", p=P)).then_inc(w_in, 16)
            with nc.allow_non_contiguous_dma(reason="short parameter vectors"):
                for j, v in enumerate((b1, gamma1, beta1)):
                    sp.dma_start(prm[:, FC * j:FC * j + FC], v.rearrange("(c p) -> p c", p=P)).then_inc(prm_in, 16)
                for j, v in enumerate((b2, gamma2, beta2)):
                    sp.dma_start(prm[:, 3 * FC + j:3 * FC + j + 1], v.rearrange("(p c) -> p c", c=1)).then_inc(prm_in, 16)
                sp.dma_start(epsb[:, :], eps.rearrange("(p c) -> p c", c=1).to_broadcast([P, 1])).then_inc(prm_in, 16)
            sp.wait_ge(h_done, len(XC))
            sp.dma_start(h_rows[0:(NBLK - 1) * P, :].rearrange("(i p) d -> p i d", p=P), hs[:, 0:NBLK - 1, :]).then_inc(h_out, 16)
            sp.dma_start(h_rows[(NBLK - 1) * P:N, :], hs[0:NREST, NBLK - 1, :]).then_inc(h_out, 16)
            sp.wait_ge(tables_ok, 1)
            sp.dma_start(tables, accf[:, 4 * NTP:6 * NTP]).then_inc(tables_out, 16)
            sp.wait_ge(h_out, 32)
            sp.wait_ge(setup_done, 1)
            slow = sp.value_load(flag[0:1, 0:1], min_val=0, max_val=8 * E)
            with sp.If(slow < 1):
                def load_step(i, u, b, kind):
                    sp.wait_ge(step_summed, i + 1)
                    sp.sem_inc(passed["sync"], 1)
                    lo = i * (T * P) + CT * P
                    if kind == "last":
                        sp.dma_start(e_gat[:, b, 0:TAILG - 1, :], edge[lo:lo + (TAILG - 1) * P, :].rearrange("(k p) d -> p k d", p=P)).then_inc(gat_e[b], 16)
                    else:
                        for h in range(2):
                            n = GT // 2
                            sp.dma_start(e_gat[:, b, h * n:(h + 1) * n, :],
                                         edge[bass.ds(lo + h * n * P, n * P), :].rearrange("(k p) d -> p k d", p=P)).then_inc(gat_e[b], 16)
                    for s in range(SETS):
                        r = (SETS * b + s) % RING
                        sp.wait_ge(ring_free, i * SETS + s + 1)
                        sp.sem_inc(passed["sync"], 1)
                        sp.dma_start(e_cnt[:, r], edge[bass.ds(i * (T * P) + s * ST * P, ST * P), :].rearrange("(k p) d -> p k d", p=P)).then_inc(cnt_landed[r], 16)
                steps(sp, load_step)
            with sp.Else():
                sp.dma_start(sd.rearrange("p a t -> p (a t)"), tables).then_inc(tables_in, 16)
                with sp.Fori(0, NG) as g:
                    sp.wait_ge(sl["added"], g * NBLK + 1)
                    sp.sem_inc(passed["sync"], 1)
                    for h in range(2):
                        n = K // 2
                        sp.dma_start(ebuf[:, h * n:(h + 1) * n, :],
                                     edge[bass.ds(g * (K * P) + h * n * P, n * P), :].rearrange("(k p) d -> p k d", p=P)).then_inc(sl["loaded"], 16)
                sp.wait_ge(sl["added"], NG * NBLK + 2)
                lo = NG * K * P
                sp.dma_start(ebuf[:, 0:TT - 1, :], edge[lo:lo + (TT - 1) * P, :].rearrange("(k p) d -> p k d", p=P)).then_inc(sl["loaded"], 16)
                sp.dma_start(ebuf[0:TREST, TT - 1, :], edge[E - TREST:E, :]).then_inc(sl["loaded"], 16)
            sp.wait_ge(sums_done, 1)
            sp.dma_start(xback[:, 0:NBLK - 1, :], x[0:(NBLK - 1) * P, :].rearrange("(i p) d -> p i d", p=P)).then_inc(back_in, 16)
            sp.dma_start(xback[0:NREST, NBLK - 1, :], x[(NBLK - 1) * P:N, :]).then_inc(back_in, 16)
            n_out = 0
            for i, blks in enumerate(HB):
                sp.wait_ge(o_ready, i + 1)
                lo, n = blks[0], len(blks)
                if blks[-1] == NBLK - 1:
                    n -= 1
                    sp.dma_start(out[(NBLK - 1) * P:N, :], otile[0:NREST, NBLK - 1, :]).then_inc(stored, 16)
                    n_out += 1
                if n:
                    sp.dma_start(out[lo * P:(lo + n) * P, :].rearrange("(i p) d -> p i d", p=P), otile[:, lo:lo + n, :]).then_inc(stored, 16)
                    n_out += 1
            sp.wait_ge(stored, 16 * n_out)

        @block.gpsimd
        def _(gp):
            def iota_to(t, pattern):
                nc.gpsimd.iota(t, pattern, base=0, channel_multiplier=0, allow_small_or_imprecise_dtypes=True).then_inc(const_ok, 1)
            nc.gpsimd.memset(ones[:, :], 1.0).then_inc(c_fill, 1)
            nc.gpsimd.memset(ones_b[:, :], 1.0)
            nc.gpsimd.memset(zero_b[:, :], 0.0)
            iota_to(zk[:, :], [[1, ZW]])
            iota_to(iota_b[:, :], [[1, P]])
            iota_to(wbase[:, :], [[P, NBLK]])
            gp.wait_ge(c_fill, 1)
            nc.gpsimd.affine_select(out=ident[:, :], in_=ones[:, :], compare_op=ALU.is_equal, fill=0.0, base=0,
                                    pattern=[[-1, P]], channel_multiplier=1).then_inc(const_ok, 1)
            nc.gpsimd.affine_select(out=ident_b[:, :], in_=ones[:, :], compare_op=ALU.is_equal, fill=0.0, base=0,
                                    pattern=[[-1, P]], channel_multiplier=1).then_inc(const_ok, 1)
            nc.gpsimd.affine_select(out=row0, in_=ones[:, :], compare_op=ALU.is_equal, fill=0.0, base=0,
                                    pattern=[[0, P]], channel_multiplier=1).then_inc(const_ok, 1)
            for j, whole in enumerate((hs, left)):
                for c, (lo, hi) in enumerate(XC):
                    gp.wait_ge(part_done, j * len(XC) + c + 1)
                    nc.gpsimd.tensor_tensor(left[:, lo:hi, :], whole[:, lo:hi, :], hp[:, j, lo:hi], ALU.subtract).then_inc(left_done, 1)
            gp.wait_ge(tables_out, 16)
            gp.wait_ge(viol_ok, 1)
            nc.gpsimd.memset(accf[:, 4 * NTP:7 * NTP], 0.0).then_inc(acc_zero, 1)
            gp.wait_ge(h_out, 32)
            gp.wait_ge(setup_done, 1)

            def gather(rows, b, k, landed, op=ALU.bypass):
                gp.indirect_dma_start(rows, None, h_rows[:, :], bass.IndirectOffsetOnAxis(ap=idx_ring[:, b, k:k + 1], axis=0),
                                      compute_op=op).then_inc(landed, 16)

            slow = gp.value_load(flag[0:1, 0:1], min_val=0, max_val=8 * E)
            with gp.If(slow < 1):
                def gather_step(i, u, b, kind):
                    gp.wait_ge(idx_ready, i + 1)
                    gp.wait_ge(gat_e[b], u * 32 + (16 if kind == "last" else 32))
                    if kind == "last":
                        gp.wait_ge(last_edges, 16)
                    gp.sem_inc(passed["gpsimd"], 1)
                    for k in range(TAILG if kind == "last" else GT):
                        gather(gathered(b, k, kind), b, k, gat_h[b], ALU.add)
                steps(gp, gather_step)
            with gp.Else():
                with gp.Fori(0, NG) as g:
                    gp.wait_ge(sl["idx"], g + 1)
                    gp.sem_inc(passed["gpsimd"], 1)
                    for k in range(K):
                        gather(gbuf[:, k, :], 0, k, sl["gathered"])
                gp.wait_ge(sl["idx"], NG + 1)
                for k in range(TT):
                    gather(gbuf[:, k, :], 0, k, sl["gathered"])
            gp.wait_ge(sums_done, 1)
            for q in range(NQ):
                cols = slice(q * Q, min(N, q * Q + Q))
                nc.gpsimd.tensor_tensor(acc[:, 0, cols], acc[:, 0, cols], acc[:, 1, cols], ALU.mult).then_inc(mean_ok, 1)

        @block.scalar
        def _(ac):
            ac.wait_ge(pads, 1)
            ac.wait_ge(idx_in, 96)
            for c, (lo, hi) in enumerate(XC):
                full = min(hi, NBLK - 1)
                ac.dma_start(xs[:, lo:full, :], x[lo * P:full * P, :].rearrange("(i p) d -> p i d", p=P)).then_inc(x_in[c], 16)
            ac.dma_start(xs[0:NREST, NBLK - 1, :], x[(NBLK - 1) * P:N, :]).then_inc(x_in[-1], 16)
            ac.wait_ge(ln_stats, 1)
            nc.scalar.activation(rstd, mv[:, :, 1], ACT.Sqrt, bias=eps_c[:, :], scale=1.0).then_inc(act_sq, 1)
            ac.wait_ge(ln_scale, 1)
            for c, (lo, hi) in enumerate(XC):
                for i in range(lo, hi):
                    last = nc.scalar.activation(hs[:, i, :], xs[:, i, :], ACT.Relu, bias=nmr[:, i:i + 1], scale=rstd[:, i:i + 1])
                last.then_inc(h_done, 1)
                ac.wait_ge(h_done, c + 1)
                nc.scalar.activation(hp[:, 0, lo:hi], hs[:, lo:hi, :], ACT.Copy).then_inc(part_done, 1)
            for j in (1, 2):
                for c, (lo, hi) in enumerate(XC):
                    ac.wait_ge(left_done, (j - 1) * len(XC) + c + 1)
                    nc.scalar.activation(hp[:, j, lo:hi], left[:, lo:hi, :], ACT.Copy).then_inc(part_done, 1)
            ac.wait_ge(setup_done, 1)
            slow = ac.value_load(flag[0:1, 0:1], min_val=0, max_val=8 * E)
            with ac.If(slow < 1):
                def count_step(i, u, b, kind):
                    ac.wait_ge(prod_done, i + 1)
                    for s in range(SETS):
                        r = (SETS * b + s) % DRING
                        ac.wait_ge(hot_ready, i * SETS + s + 1)
                        nc.scalar.activation(dhot_b[:, r], dhot[:, r], ACT.Copy).then_inc(dcopy_ready, 1)
                        if s == SETS - 1:
                            g = TAILG if kind == "last" else GT
                            ac.wait_ge(ghot_ready, i + 1)
                            nc.scalar.activation(ghot_b[:, 0:g], ghot[:, 0:g], ACT.Copy).then_inc(gcopy_ready, 1)
                        ac.wait_ge(set_free, i * SETS + s + 3)
                        for j in range(AB):
                            n = min(AR, NBLK - j * AR)
                            last = nc.scalar.activation(cnt[:, b, j * AR:j * AR + n, s * WS:(s + 1) * WS],
                                                        set_ps[(SETS * b + s) % 2][j][:, 0:n, :], ACT.Copy)
                        last.then_inc(cnt_ready, 1)
                steps(ac, count_step)
            t = 0
            for q in range(NQ):
                for c in range(FC):
                    n = min(Q, N - q * Q)
                    ac.wait_ge(mm1, t + 1)
                    nc.scalar.activation(y1[:, c, q * Q:q * Q + n], bank[4 + t % 4][:, 0:n], ACT.Identity,
                                         bias=prm[:, c:c + 1], scale=1.0).then_inc(y_out, 1)
                    t += 1
            ac.wait_ge(bn_stat, 1)
            nc.scalar.activation(bsc[:, :, 2], bmv[:, :, 1], ACT.Sqrt, bias=eps_c[:, :], scale=1.0).then_inc(act_sq, 1)
            ac.wait_ge(bn_coef, 1)
            for q in range(NQ):
                for c in range(FC):
                    n = min(Q, N - q * Q)
                    nc.scalar.activation(y1[:, c, q * Q:q * Q + n], y1[:, c, q * Q:q * Q + n], ACT.Relu,
                                         bias=bsc[:, c, 1:2], scale=bsc[:, c, 0:1]).then_inc(y_norm, 1)
            ac.wait_ge(bn_stat, 2)
            nc.scalar.activation(bsc[:, 0:1, 2], bmv[:, 0:1, 1], ACT.Sqrt, bias=eps_c[:, :], scale=1.0).then_inc(act_sq, 1)
            ac.wait_ge(bn_coef, 2)
            for q in range(NQ):
                n = min(Q, N - q * Q)
                nc.scalar.activation(y2[:, q * Q:q * Q + n], y2[:, q * Q:q * Q + n], ACT.Relu,
                                     bias=bsc[:, 0, 1:2], scale=bsc[:, 0, 0:1]).then_inc(y_norm, 1)

        @block.vector
        def _(ve):
            n_chain = [0]

            def link(ins):
                n_chain[0] += 1
                ins.then_inc(chain, 1)
                ve.wait_ge(chain, n_chain[0])

            nc.vector.memset(xs[:, NBLK - 1, :], 0.0)
            nc.vector.memset(e_last[:, :], 0.0).then_inc(pads, 1)
            nc.vector.memset(raw_i[:, 0, NCH - 1, :], 0)
            nc.vector.memset(raw_i[:, 1, NCH - 1, :], PAD).then_inc(pads, 1)
            nc.vector.memset(eps_c[:, :], LN_EPS)
            ve.wait_ge(idx_in, 96)
            nc.vector.tensor_scalar(raw_i[:, 2], raw_i[:, 0], 7, None, ALU.logical_shift_right)
            link(nc.vector.tensor_scalar(raw_i[:, 3], raw_i[:, 0], P - 1, None, ALU.bitwise_and))
            nc.vector.tensor_copy(raw_f[:, :], raw_i[:, 1:4]).then_inc(idx_float, 1)
            for c, (lo, hi) in enumerate(XC):
                ve.wait_ge(x_in[c], 32 if hi == NBLK else 16)
                for i in range(lo, hi):
                    last = nc.vector.bn_stats(stats[:, i, :], xs[:, i, :])
            link(last)
            for i in range(NBLK):
                last = nc.vector.bn_aggr(mv[:, i, :], stats[:, i, :])
            last.then_inc(ln_stats, 1)
            ve.wait_ge(act_sq, 1)
            link(nc.vector.reciprocal(rstd, rstd))
            nc.vector.scalar_tensor_tensor(out=nmr, in0=mv[:, :, 0], scalar=-1.0, in1=rstd,
                                           op0=ALU.mult, op1=ALU.mult).then_inc(ln_scale, 1)
            for n, (a, cs) in enumerate(IB):
                ve.wait_ge(idx_bank, n + 1)
                w = len(cs) * P
                last = nc.vector.tensor_copy(idxT[:, a, cs[0] * P:cs[0] * P + w], bank[4 + n % 4][:, 0:w])
                last.then_inc(idx_taken, 1)
            ve.wait_ge(firsts, 1)
            bt, relf, chk = tmp
            link(nc.vector.tensor_copy(bt, psf[:, 0:NTP]))
            link(nc.vector.tensor_tensor(relf, idxT[:, 0], bt, ALU.subtract))
            nc.vector.tensor_copy(row[:, :], idxT[:, 2])
            nc.vector.scalar_tensor_tensor(out=key[:, :], in0=idxT[:, 1], scalar=float(WT), in1=relf, op0=ALU.mult, op1=ALU.add)
            link(nc.vector.scalar_tensor_tensor(out=idxT[:, 1], in0=idxT[:, 1], scalar=float(P), in1=idxT[:, 2], op0=ALU.mult, op1=ALU.add))
            nc.vector.tensor_copy(gat_src[:, :, :], idxT[:, 1, 0:(NSTEP + 1) * T].rearrange("p (i t) -> p i t", t=T)[:, :, CT:T]).then_inc(tables_ok, 1)
            nc.vector.tensor_reduce(ext[:, 0:1], relf[:, 0:NT - 1], axis=AX.X, op=ALU.max)
            nc.vector.tensor_reduce(ext[:, 1:2], relf[:, 0:NT], axis=AX.X, op=ALU.min)
            link(nc.vector.tensor_scalar(viol[:, 0:1], relf[:, NT - 1:NT], float(WT), None, ALU.is_ge))
            link(nc.vector.scalar_tensor_tensor(out=viol[:, 0:1], in0=relf[:, NT - 1:NT], scalar=PAD / 2.0, in1=viol[:, 0:1], op0=ALU.is_lt, op1=ALU.mult))
            TI = (NSTEP + 1) * T
            link(nc.vector.tensor_copy(idxT[:, 2], relf))
            btv = bt[:, 0:TI].rearrange("p (i t) -> p i t", t=T)
            offv = relf[:, 0:TI].rearrange("p (i t) -> p i t", t=T)
            for s in range(SETS):
                nc.vector.tensor_tensor(offv[:, :, s * ST:(s + 1) * ST], btv[:, :, s * ST:(s + 1) * ST],
                                        btv[:, :, s * ST:s * ST + 1].to_broadcast([P, NSTEP + 1, ST]), ALU.subtract)
            link(nc.vector.tensor_tensor(offv[:, :, CT:T], btv[:, :, CT:T], btv[:, :, CT:CT + 1].to_broadcast([P, NSTEP + 1, GT]), ALU.subtract))
            nc.vector.tensor_copy(base_i[:, :].rearrange("p (i s) -> p i s", s=NBASE), btv[:, :, 0:CT + 1:ST])
            nc.vector.tensor_copy(off_i[:, :].rearrange("p (i t) -> p i t", t=CT), offv[:, :, 0:CT])
            nc.vector.tensor_tensor(rel[:, 0:TI], relf[:, 0:TI], idxT[:, 2, 0:TI], ALU.add)
            n_set = (NSTEP + 1) * SETS * (ST - 1)
            in_set = offv[:, :, 0:CT].rearrange("p i (s k) -> p i s k", s=SETS)
            nc.vector.tensor_tensor(chk[:, 0:n_set].rearrange("p (i s k) -> p i s k", s=SETS, k=ST - 1), in_set[:, :, :, 1:ST],
                                    in_set[:, :, :, 0:ST - 1], ALU.subtract)
            n_gat = (NSTEP + 1) * (GT - 1)
            link(nc.vector.tensor_tensor(chk[:, n_set:n_set + n_gat].rearrange("p (i k) -> p i k", k=GT - 1), offv[:, :, CT + 1:T],
                                         offv[:, :, CT:T - 1], ALU.subtract))
            nc.vector.tensor_reduce(ext[:, 2:3], chk[:, 0:n_set + n_gat], axis=AX.X, op=ALU.min)
            nc.vector.tensor_reduce(ext[:, 3:4], chk[:, 0:n_set], axis=AX.X, op=ALU.max)
            nc.vector.tensor_reduce(ext[:, 4:5], offv[:, :, ST - 1:CT:ST], axis=AX.XY, op=ALU.max)
            nc.vector.tensor_reduce(ext[:, 5:6], offv[:, :, ST - 1:CT:ST], axis=AX.XY, op=ALU.min)
            nc.vector.tensor_reduce(ext[:, 6:7], offv[:, 0:NSTEP, T - 1:T], axis=AX.XY, op=ALU.max)
            ve.wait_ge(const_ok, 6)
            link(nc.vector.tensor_tensor(ahead[:, :], bt[:, 2 * T:NSTEP * T:2 * T], wbase[:, 3:3 * (NSTEP // 2):3], ALU.subtract))
            link(nc.vector.tensor_reduce(ext[:, 7:8], ahead[:, :], axis=AX.X, op=ALU.min))
            for j, (value, limit, op) in enumerate((
                    (ext[:, 0:1], WT, ALU.is_ge), (ext[:, 1:2], 0, ALU.is_lt), (ext[:, 2:3], 0, ALU.is_lt), (ext[:, 3:4], WT, ALU.is_gt),
                    (ext[:, 4:5], WS - WT, ALU.is_gt), (ext[:, 5:6], COVER - WT, ALU.is_lt), (ext[:, 6:7], WG - WT, ALU.is_gt),
                    (ext[:, 7:8], 0, ALU.is_lt),
                    (offv[:, NSTEP, CT + TAILG - 1:CT + TAILG], WG - WT, ALU.is_gt))):
                last = nc.vector.tensor_scalar(viol[:, j + 1:j + 2], value, float(limit), None, op)
            link(last)
            nc.vector.tensor_reduce(viol[:, 10:11], viol[:, 0:10], axis=AX.X, op=ALU.add).then_inc(viol_ok, 1)
            ve.wait_ge(viol_ok, 1)
            nc.vector.memset(accf[:, 0:4 * NTP], 0.0)
            link(nc.vector.memset(accf[:, 7 * NTP:2 * NACC], 0.0))
            ve.wait_ge(viol_sum, 1)
            link(nc.vector.tensor_copy(flag[:, :], bank[4][:, 0:1]))
            ve.wait_ge(const_ok, 6)
            ve.wait_ge(part_done, 3 * len(XC))
            ve.wait_ge(acc_zero, 1)
            ve.sem_inc(setup_done, 1)

            def invert(cols, before):
                nc.vector.tensor_scalar(acc[:, 1, cols], acc[:, 1, cols], 1.0, None, ALU.max).then_inc(inverted, 1)
                ve.wait_ge(inverted, before + 1)
                ve.sem_inc(passed["vector"], 1)
                nc.vector.reciprocal(acc[:, 1, cols], acc[:, 1, cols]).then_inc(inverted, 1)

            slow = ve.value_load(flag[0:1, 0:1], min_val=0, max_val=8 * E)
            with ve.If(slow < 1):
                for s_, credit in ((set_free, 2), (cnt_ready, 2), (ring_free, RING), (step_summed, 2), (prod_done, 2),
                                   (sums_taken, 2), (acc_add, 1)):
                    ve.sem_inc(s_, credit)
                nc.vector.tensor_copy(idx_ring[:, 0, :], gat_src[:, 0, :]).then_inc(idx_ready, 1)
                def add_sums(i, b, finished, drain=False):
                    base = nc.values_load_multi_w_load_instructions(base_i[0:1, bass.ds(i * NBASE, NBASE)], engines=(DVE_ENGINE,),
                                                                    min_val=0, max_val=N - 1)[1]
                    ve.wait_ge(finished, i + 3)
                    for s in range(NBASE):
                        w = WS if s < SETS else WG
                        a = acc[:, :, bass.ds(base[s], w)]
                        ve.wait_ge(acc_add, i * NBASE + s + 1)
                        nc.vector.tensor_tensor(a, a, sums[b][:, :, s * WS:s * WS + w], ALU.add).then_inc(acc_add, 1)
                    ve.wait_ge(acc_add, i * NBASE + NBASE + 1)
                    if not drain:
                        nc.vector.memset(sums[b][:, :, 0:SETS * WS + WG], 0.0).then_inc(sums_taken, 1)
                    return base

                def hots(i, b, s):
                    ve.wait_ge(set_free, i * SETS + s + 1)
                    r = (SETS * b + s) % DRING
                    nc.vector.tensor_tensor(dhot[:, r], iota_b[:, 0:WS].unsqueeze(1).to_broadcast([P, ST, WS]),
                                            rel[:, bass.ds(i * T + s * ST, ST)].unsqueeze(2).to_broadcast([P, ST, WS]), ALU.is_equal)
                    for k in range(ST):
                        t = i * T + (s * ST + k)
                        nc.vector.tensor_scalar(zhot[:, (SETS * b + s) % 2, k, :], zk[:, :], key[:, bass.ds(t, 1)], None, ALU.is_equal)
                        last = nc.vector.tensor_scalar(rhot[:, (SETS * b + s) % 2, k, :], zk[:, 0:P], row[:, bass.ds(t, 1)], None, ALU.is_equal)
                    last.then_inc(hot_ready, 1)

                def one_step(i, u, b, kind):
                    g = TAILG if kind == "last" else GT
                    hots(i, b, 0)
                    hots(i, b, 1)
                    if kind not in ("first", "second"):
                        add_sums(i - 2, b, prod_done)
                    if kind != "last":
                        ve.wait_ge(step_summed, i + 2)
                        ve.sem_inc(passed["vector"], 1)
                        nc.vector.tensor_copy(idx_ring[:, 1 - b, :], gat_flat[:, bass.ds(i * GT + GT, GT)]).then_inc(idx_ready, 1)
                    hots(i, b, 2)
                    hots(i, b, 3)
                    ve.wait_ge(step_summed, i + 2)
                    nc.vector.tensor_tensor(ghot[:, 0:g, :], iota_b[:, 0:WG].unsqueeze(1).to_broadcast([P, g, WG]),
                                            rel[:, bass.ds(i * T + CT, g)].unsqueeze(2).to_broadcast([P, g, WG]), ALU.is_equal).then_inc(ghot_ready, 1)
                    for s in range(4, SETS):
                        hots(i, b, s)
                    if kind == "whole" and b == 1:
                        invert(bass.ds(u * CH - CH, CH), u * 2 - 2)
                steps(ve, one_step)
                add_sums(NSTEP - 1, 1, prod_done, drain=True)
                base = add_sums(NSTEP, 0, step_summed, drain=True)
                n_inv = 2 * (NSTEP // 2 - 1)
                invert(slice(DONE, N), n_inv)
                ve.wait_ge(prod_done, NSTEP + 3)
                for s in range(SETS):
                    a = acc[:, 0, bass.ds(base[s], WS)]
                    ve.wait_ge(acc_add, (NSTEP + 1) * NBASE + s + 1)
                    nc.vector.tensor_tensor(a, a, last_prod[:, s * WS:(s + 1) * WS], ALU.add).then_inc(acc_add, 1)
                ve.wait_ge(acc_add, (NSTEP + 1) * NBASE + SETS + 1)
                ve.wait_ge(inverted, n_inv + 2)
                ve.sem_inc(sums_done, 1)
            with ve.Else():
                ve.wait_ge(tables_in, 16)
                ve.wait_ge(last_edges, 16)
                ve.sem_inc(sl["added"], 1)

                def window(g, w, tiles, dests):
                    nth = g * NBLK + w
                    nc.vector.tensor_copy(rel_w[:, 0:tiles], dests).then_inc(sl["step"], 1)
                    ve.wait_ge(sl["step"], nth * 2 + 1)
                    nc.vector.tensor_tensor(rel_w[:, 0:tiles], rel_w[:, 0:tiles], wbase[:, bass.ds(w, 1)].to_broadcast([P, tiles]),
                                            ALU.subtract).then_inc(sl["step"], 1)
                    ve.wait_ge(sl["step"], nth * 2 + 2)
                    nc.vector.tensor_tensor(onehot[:, 0:tiles, :], iota_b[:, :].unsqueeze(1).to_broadcast([P, tiles, P]),
                                            rel_w[:, 0:tiles].unsqueeze(2).to_broadcast([P, tiles, P]), ALU.is_equal).then_inc(sl["onehot"], 1)
                    ve.wait_ge(sl["mm"], nth + 1)
                    for j in range(2):
                        a = acc[:, j, bass.ds(w * P, P)]
                        last = nc.vector.tensor_tensor(a, a, bank[6 + j][:, 0:P], ALU.add)
                    return last

                with ve.Fori(0, NG) as g:
                    nc.vector.tensor_copy(idx_ring[:, 0, 0:K], sd[:, 1, bass.ds(g * K, K)]).then_inc(sl["idx"], 1)
                    with ve.Fori(0, NBLK) as w:
                        window(g, w, K, sd[:, 0, bass.ds(g * K, K)]).then_inc(sl["added"], 1)
                        ve.wait_ge(sl["added"], g * NBLK + w + 2)
                nc.vector.memset(ebuf[:, TT - 1, :], 0.0).then_inc(sl["added"], 1)
                nc.vector.tensor_copy(idx_ring[:, 0, 0:TT], sd[:, 1, NG * K:NT]).then_inc(sl["idx"], 1)
                with ve.Fori(0, NBLK) as w:
                    window(NG, w, TT, sd[:, 0, NG * K:NT]).then_inc(sl["tail"], 1)
                    ve.wait_ge(sl["tail"], w + 1)
                invert(slice(0, N), 0)
                ve.wait_ge(inverted, 2)
                ve.sem_inc(sums_done, 1)

            ve.wait_ge(prm_in, 112)
            link(nc.vector.tensor_scalar(epsb[:, :], epsb[:, :], 1.0, None, ALU.add))

            def stat_chunk(q):
                n = min(Q, N - q * Q)
                for c in range(FC):
                    ve.wait_ge(y_out, q * FC + c + 1)
                    last = nc.vector.bn_stats(bstat[:, c, q, :], y1[:, c, q * Q:q * Q + n])
                return last

            def add_h(q):
                n = min(Q, N - q * Q)
                ve.wait_ge(mean_ok, q + 1)
                ve.wait_ge(zT, q + 1)
                nc.vector.scalar_tensor_tensor(out=acc[:, 0, q * Q:q * Q + n], in0=bank[q % 4][:, 0:n], scalar=epsb[:, :],
                                               in1=acc[:, 0, q * Q:q * Q + n], op0=ALU.mult, op1=ALU.add).then_inc(z_ready, 1)

            for q in range(NQ):
                add_h(q)
                if q >= 2:
                    stat_chunk(q - 2)
            stat_chunk(NQ - 2)
            last = stat_chunk(NQ - 1)

            def scale_shift(last, nch, pg, pb, sq):
                link(last)
                for cc in range(nch):
                    last = nc.vector.bn_aggr(bmv[:, cc, :], bstat[:, cc, :, :].rearrange("p q s -> p (q s)"))
                last.then_inc(bn_stat, 1)
                ve.wait_ge(act_sq, sq)
                link(nc.vector.reciprocal(bsc[:, 0:nch, 2], bsc[:, 0:nch, 2]))
                link(nc.vector.tensor_tensor(bsc[:, 0:nch, 0], prm[:, pg:pg + nch], bsc[:, 0:nch, 2], ALU.mult))
                link(nc.vector.tensor_tensor(bsc[:, 0:nch, 1], bmv[:, 0:nch, 0], bsc[:, 0:nch, 0], ALU.mult))
                nc.vector.tensor_tensor(bsc[:, 0:nch, 1], prm[:, pb:pb + nch], bsc[:, 0:nch, 1], ALU.subtract).then_inc(bn_coef, 1)

            scale_shift(last, FC, FC, 2 * FC, 2)
            for q in range(NQ):
                n = min(Q, N - q * Q)
                ve.wait_ge(mm2, q + 1)
                nc.vector.tensor_scalar(y2[:, q * Q:q * Q + n], bank[q % 8][:, 0:n], prm[:, 3 * FC:3 * FC + 1], None, ALU.add).then_inc(y2_out, 1)
                ve.wait_ge(y2_out, q + 1)
                last = nc.vector.bn_stats(bstat[:, 0, q, :], y2[:, q * Q:q * Q + n])
            scale_shift(last, 1, 3 * FC + 1, 3 * FC + 2, 3)
            ve.wait_ge(back_in, 32)
            for i, blks in enumerate(HB):
                ve.wait_ge(o_T, i + 1)
                w = len(blks) * P
                lo = blks[0]
                rows = NREST if blks == [NBLK - 1] else P
                nc.vector.tensor_tensor(otile[0:rows, lo:lo + len(blks), :], xback[0:rows, lo:lo + len(blks), :],
                                        bank[i % 8][0:rows, 0:w].rearrange("p (i d) -> p i d", d=D), ALU.add).then_inc(o_ready, 1)

        @block.tensor
        def _(te):
            te.wait_ge(const_ok, 6)
            te.wait_ge(idx_float, 1)
            for n, (a, cs) in enumerate(IB):
                if n >= 4:
                    te.wait_ge(idx_taken, n - 3)
                for j, c in enumerate(cs):
                    last = nc.tensor.transpose(bank[4 + n % 4][:, j * P:(j + 1) * P], raw_f[:, a, c, :], ident[:, :])
                last.then_inc(idx_bank, 1)
            te.wait_ge(idx_taken, len(IB))
            for q in range(0, NTP, Q):
                n = min(Q, NTP - q)
                last = nc.tensor.matmul(psf[:, q:q + n], row0, idxT[:, 0, q:q + n], start=True, stop=True)
            last.then_inc(firsts, 1)
            te.wait_ge(viol_ok, 1)
            nc.tensor.matmul(bank[4][:, 0:1], ones[:, :], viol[:, 10:11], start=True, stop=True).then_inc(viol_sum, 1)
            te.wait_ge(setup_done, 1)
            slow = te.value_load(flag[0:1, 0:1], min_val=0, max_val=8 * E)
            with te.If(slow < 1):
                for j in (6, 7):
                    for h in range(2):
                        nc.tensor.matmul(bank[j][:, h * Q // 2:(h + 1) * Q // 2], zero_b[:, :], zk[:, 0:Q // 2], start=(h == 0), stop=True,
                                         skip_group_check=True)

                def places(t, n, most):
                    return nc.values_load_multi_w_load_instructions(off_i[0:1, bass.ds(t, n)], engines=(PE_ENGINE,),
                                                                    min_val=0, max_val=most - WT,
                                                                    skip_runtime_bounds_check_because="the flag says that all places fit")[1]

                def count(i, u, b, s, between):
                    offs = places(i * CT + s * ST, ST, WS)
                    te.wait_ge(cnt_ready, i * SETS + s + 1)
                    te.wait_ge(hot_ready, i * SETS + s + 1)
                    for j in range(AB):
                        nc.tensor.matmul(set_ps[(SETS * b + s) % 2][j][:, :, COVER:WS], zero_b[:, :],
                                         zk[:, 0:AR * (WS - COVER)].rearrange("p (a w) -> p a w", a=AR),
                                         start=True, stop=False, skip_group_check=True)
                    for k in range(ST):
                        for j in range(AB):
                            o = set_ps[(SETS * b + s) % 2][j]
                            o = o[:, :, 0:WT] if k == 0 else o[:, :, bass.ds(offs[k], WT)]
                            last = nc.tensor.matmul(o, rhot[:, (SETS * b + s) % 2, k, :],
                                                    zhot[:, (SETS * b + s) % 2, k, j * AR * WT:(j + 1) * AR * WT].rearrange("p (a w) -> p a w", a=AR),
                                                    start=False, stop=(k == ST - 1), skip_group_check=True)
                        if k == ST - 1:
                            last.then_inc(set_free, 1)
                        between(PER_COUNT[k % 2])

                def sum_tile(b, col, edges, hot, hot_b):
                    w = hot.shape[-1]
                    nc.tensor.matmul(sums[b][:, 0, col:col + w], edges, hot, start=False, stop=True, skip_group_check=True)
                    return nc.tensor.matmul(sums[b][:, 1, col:col + w], ones_b[:, :], hot_b, start=False, stop=True, skip_group_check=True)

                def sum_set(i, u, b, s, between):
                    if s == 0:
                        te.wait_ge(sums_taken, i + 1)
                    r, d = (SETS * b + s) % RING, (SETS * b + s) % DRING
                    te.wait_ge(cnt_landed[r], u * (16 * 2 * SETS // RING) + ((SETS * b + s) // RING + 1) * 16)
                    te.wait_ge(dcopy_ready, i * SETS + s + 1)
                    for k in range(ST):
                        last = sum_tile(b, s * WS, e_cnt[:, r, k, :], dhot[:, d, k, :], dhot_b[:, d, k, :])
                        if k == ST - 1:
                            last.then_inc(ring_free, 1)
                        between(PER_SUM)

                def product(i, b, out):
                    todo = [(a, j) for a in range(NBLK) for j in range(3)]

                    def some(n):
                        if len(todo) == 3 * NBLK:
                            te.wait_ge(cnt_ready, i * SETS + (SETS + 2))
                        for a, j in todo[:n]:
                            last = nc.tensor.matmul(out, hp[:, j, a, :], cnt[:, b, a, :], start=(out is last_prod and a + j == 0), stop=True, skip_group_check=True)
                        if todo and n >= len(todo):
                            last.then_inc(prod_done, 1)
                        del todo[:n]
                    return some

                def pe_step(i, u, b, kind):
                    between = (lambda n: None) if kind == "first" else product(i - 1, 1 - b, sums[1 - b][:, 0, 0:WC])
                    count(i, u, b, 0, between)
                    for s in range(1, SETS):
                        count(i, u, b, s, between)
                        sum_set(i, u, b, s - 1, between)
                    sum_set(i, u, b, SETS - 1, between)
                    g = TAILG if kind == "last" else GT
                    te.wait_ge(gat_h[b], u * (16 * GT) + 16 * g)
                    te.wait_ge(gcopy_ready, i + 1)
                    for k in range(g):
                        last = sum_tile(b, SETS * WS, gathered(b, k, kind), ghot[:, k, :], ghot_b[:, k, :])
                        if k == g - 1:
                            last.then_inc(step_summed, 1)
                        between(PER_GATHERED)
                    between(3 * NBLK)
                steps(te, pe_step)
                product(NSTEP, 0, last_prod)(3 * NBLK)
            with te.Else():
                def group(tiles):
                    for k in range(tiles):
                        nc.tensor.matmul(bank[6][:, 0:P], ebuf[:, k, :], onehot[:, k, :], start=(k == 0), stop=False)
                        nc.tensor.matmul(bank[6][:, 0:P], gbuf[:, k, :], onehot[:, k, :], start=False, stop=(k == tiles - 1))
                        last = nc.tensor.matmul(bank[7][:, 0:P], ones[:, :], onehot[:, k, :], start=(k == 0), stop=(k == tiles - 1))
                    return last
                with te.Fori(0, NG) as g:
                    te.wait_ge(sl["loaded"], g * 32 + 32)
                    te.wait_ge(sl["gathered"], g * (16 * K) + 16 * K)
                    te.sem_inc(passed["tensor"], 1)
                    with te.Fori(0, NBLK) as w:
                        te.wait_ge(sl["onehot"], g * NBLK + w + 1)
                        group(K).then_inc(sl["mm"], 1)
                te.wait_ge(sl["loaded"], NG * 32 + 32)
                te.wait_ge(sl["gathered"], NG * 16 * K + 16 * TT)
                with te.Fori(0, NBLK) as w:
                    te.wait_ge(sl["onehot"], w + (NG * NBLK + 1))
                    group(TT).then_inc(sl["mm"], 1)

            def layer1(q):
                te.wait_ge(z_ready, q + 1)
                n = min(Q, N - q * Q)
                for c in range(FC):
                    t = q * FC + c
                    if t >= 4:
                        te.wait_ge(y_out, t - 3)
                    nc.tensor.matmul(bank[4 + t % 4][:, 0:n], w1s[:, c * P:(c + 1) * P], acc[:, 0, q * Q:q * Q + n],
                                     start=True, stop=True).then_inc(mm1, 1)

            te.wait_ge(w_in, 32)
            for q in range(NQ):
                if q >= 4:
                    te.wait_ge(z_ready, q - 3)
                for j, c in enumerate(HB[q]):
                    for p_ in range(3):
                        last = nc.tensor.matmul(bank[q % 4][:, j * P:(j + 1) * P], hp[:, p_, c, :], ident_b[:, :],
                                                start=(p_ == 0), stop=(p_ == 2))
                last.then_inc(zT, 1)
                if q:
                    layer1(q - 1)
            layer1(NQ - 1)
            te.wait_ge(y_out, NQ * FC)
            for q in range(NQ):
                n = min(Q, N - q * Q)
                te.wait_ge(y_norm, (q + 1) * FC)
                if q >= 8:
                    te.wait_ge(y2_out, q - 7)
                for c in range(FC):
                    last = nc.tensor.matmul(bank[q % 8][:, 0:n], w2s[:, c, :], y1[:, c, q * Q:q * Q + n],
                                            start=(c == 0), stop=(c == FC - 1))
                last.then_inc(mm2, 1)
            te.wait_ge(y2_out, NQ)
            for i, blks in enumerate(HB):
                te.wait_ge(y_norm, NQ * FC + i + 1)
                if i >= 8:
                    te.wait_ge(o_ready, i - 7)
                for j, c in enumerate(blks):
                    w = min(P, N - c * P)
                    last = nc.tensor.transpose(bank[i % 8][0:w, j * P:(j + 1) * P], y2[:, c * P:c * P + w], ident[:, :])
                last.then_inc(o_T, 1)


_INS = ['x', 'src', 'dst', 'edge_attr_128', 'L0_gnn_eps', 'L0_gnn_W1', 'L0_gnn_b1', 'L0_gnn_gamma1', 'L0_gnn_beta1',
        'L0_gnn_W2', 'L0_gnn_b2', 'L0_gnn_gamma2', 'L0_gnn_beta2']


def kernel(**inputs):
    import numpy as _np
    import concourse.bacc as _bacc
    from concourse import mybir as _mybir
    from concourse.bass_utils import run_bass_kernel_spmd as _run

    nc = _bacc.Bacc("TRN2", target_bir_lowering=False, num_devices=1)
    arrays, args = {}, []
    for name in _INS:
        a = _np.ascontiguousarray(inputs[name])
        arrays[f"in_{name}"] = a
        args.append(nc.dram_tensor(f"in_{name}", a.shape, _mybir.dt.from_np(a.dtype), kind="ExternalInput").ap())
    shape = inputs['x'].shape
    args.append(nc.dram_tensor("out_x", shape, _mybir.dt.float32, kind="ExternalOutput").ap())
    args.append(nc.dram_tensor("h_rows", shape, _mybir.dt.float32, kind="Internal").ap())
    n_tables = 2 * (-(-inputs['src'].shape[0] // 128 ** 2)) * 128
    args.append(nc.dram_tensor("tables", (128, n_tables), _mybir.dt.float32, kind="Internal").ap())
    gnn_layer(nc, *args)
    r = _run(nc, [arrays], core_ids=[0])
    return r.results[0]["out_x"]
```
